# Optimizing a Trainium2 kernel written in Bass

```python
import numpy as np
import jax
import jax.numpy as jnp

def _softmax(x, axis=-1):
    return jax.nn.softmax(x, axis=axis)

def _gelu(x):
    return jax.nn.gelu(x, approximate=True)

def _silu(x):
    return jax.nn.silu(x)

def _sigmoid(x):
    return jax.nn.sigmoid(x)

def _layernorm(x, axis=-1, eps=1e-05):
    m = jnp.mean(x, axis=axis, keepdims=True)
    v = jnp.var(x, axis=axis, keepdims=True)
    return (x - m) / jnp.sqrt(v + eps)

def _scatter_add(tgt, idx, src, axis=0):
    return tgt.at[idx].add(src)

def _segment_sum(src, seg, n):
    return jax.ops.segment_sum(src, seg, n)
kernel_name = 'mk_adj_resnorm_d2_adj_r2_5961ea'

def setup_inputs(seed: int=0):
    np.random.seed(seed)
    _w = jnp.asarray

    def _rec_inputs():
        import jax
        import jax.numpy as jnp
        _gk = jax.random.key(seed)
        x = 0.0002141 + 1 * jax.random.normal(jax.random.fold_in(_gk, 1), (8192, 64), jnp.float32)
        _a = jax.random.bernoulli(jax.random.fold_in(_gk, 2), 0.000488281, (8192, 8192))
        _af = _a.astype(jnp.float32)
        adj = _af
        return (x, adj)
    x, adj = _rec_inputs()

    def _L0_gnn_setup():
        import jax, jax.numpy as jnp
        import numpy as np
        import math
        N = 6144
        D = 64
        SCALE0 = math.log(10.0)

        def lorentz_linear(x, W, b, scale):
            h = x @ W.T + b
            time = jax.nn.sigmoid(h[:, :1]) * jnp.exp(scale) + 1.1
            xn = h[:, 1:]
            sq = jnp.clip(jnp.sum(xn * xn, axis=-1, keepdims=True), 1e-08, None)
            s = (time * time - 1.0) / sq
            return jnp.concatenate([time, xn * jnp.sqrt(s)], axis=-1)
        key = jax.random.key(seed)
        ks = jax.random.split(key, 8)
        stdv = 1.0 / math.sqrt(D)
        x = jax.random.normal(ks[0], (N, D), dtype=jnp.float32)
        adj = (jax.random.uniform(ks[1], (N, N)) < 0.002).astype(jnp.float32)
        W = jax.random.uniform(ks[2], (D, D), minval=-stdv, maxval=stdv, dtype=jnp.float32)
        Wq = jax.random.uniform(ks[3], (D, D), minval=-stdv, maxval=stdv, dtype=jnp.float32)
        Wk = jax.random.uniform(ks[4], (D, D), minval=-stdv, maxval=stdv, dtype=jnp.float32)
        z = jnp.zeros((D,), dtype=jnp.float32)
        sc = jnp.asarray(SCALE0, dtype=jnp.float32)
        return {'x': x, 'adj': adj, 'W': W, 'b': z, 'scale': sc, 'Wq': Wq, 'bq': z, 'scale_q': sc, 'Wk': Wk, 'bk': z, 'scale_k': sc, 'att_bias': jnp.asarray(20.0, dtype=jnp.float32), 'att_scale': jnp.asarray(math.sqrt(D), dtype=jnp.float32)}
    _L0_gnn_all = _L0_gnn_setup()
    _L0_gnn_in = {k: v for k, v in _L0_gnn_all.items() if k in ('W', 'b', 'scale', 'Wq', 'bq', 'scale_q', 'Wk', 'bk', 'scale_k', 'att_bias', 'att_scale')}
    del _L0_gnn_all

    def _L1_gnn_setup():
        import jax, jax.numpy as jnp
        import numpy as np
        N, D_IN, D_OUT = (8192, 64, 64)
        AVG_DEG = 32.0
        L2_EPS = 1e-12
        key = jax.random.key(seed)
        kx, ka, kw, kb = jax.random.split(key, 4)
        X = jax.random.normal(kx, (N, D_IN), dtype=jnp.float32)
        adj = (jax.random.uniform(ka, (N, N)) < AVG_DEG / N).astype(jnp.float32)
        bound = 1.0 / np.sqrt(2 * D_IN)
        W = jax.random.uniform(kw, (2 * D_IN, D_OUT), dtype=jnp.float32, minval=-bound, maxval=bound)
        b = jax.random.uniform(kb, (D_OUT,), dtype=jnp.float32, minval=-bound, maxval=bound)
        return {'X': X, 'adj': adj, 'W': W, 'b': b}
    _L1_gnn_all = _L1_gnn_setup()
    _L1_gnn_in = {k: v for k, v in _L1_gnn_all.items() if k in ('W', 'b')}
    del _L1_gnn_all
    return {'x': x, 'adj': adj, 'L0_gnn_W': _L0_gnn_in['W'], 'L0_gnn_b': _L0_gnn_in['b'], 'L0_gnn_scale': _L0_gnn_in['scale'], 'L0_gnn_Wq': _L0_gnn_in['Wq'], 'L0_gnn_bq': _L0_gnn_in['bq'], 'L0_gnn_scale_q': _L0_gnn_in['scale_q'], 'L0_gnn_Wk': _L0_gnn_in['Wk'], 'L0_gnn_bk': _L0_gnn_in['bk'], 'L0_gnn_scale_k': _L0_gnn_in['scale_k'], 'L0_gnn_att_bias': _L0_gnn_in['att_bias'], 'L0_gnn_att_scale': _L0_gnn_in['att_scale'], 'L1_gnn_W': _L1_gnn_in['W'], 'L1_gnn_b': _L1_gnn_in['b']}

def reference(x, adj, L0_gnn_W, L0_gnn_b, L0_gnn_scale, L0_gnn_Wq, L0_gnn_bq, L0_gnn_scale_q, L0_gnn_Wk, L0_gnn_bk, L0_gnn_scale_k, L0_gnn_att_bias, L0_gnn_att_scale, L1_gnn_W, L1_gnn_b):
    import jax
    import jax.numpy as jnp

    def _L0_gnn_ref(x, adj, W, b, scale, Wq, bq, scale_q, Wk, bk, scale_k, att_bias, att_scale):
        import jax, jax.numpy as jnp
        import numpy as np
        import math
        N = 6144
        D = 64
        SCALE0 = math.log(10.0)

        def lorentz_linear(x, W, b, scale):
            h = x @ W.T + b
            time = jax.nn.sigmoid(h[:, :1]) * jnp.exp(scale) + 1.1
            xn = h[:, 1:]
            sq = jnp.clip(jnp.sum(xn * xn, axis=-1, keepdims=True), 1e-08, None)
            s = (time * time - 1.0) / sq
            return jnp.concatenate([time, xn * jnp.sqrt(s)], axis=-1)
        h = lorentz_linear(x, W, b, scale)
        q = lorentz_linear(h, Wq, bq, scale_q)
        k = lorentz_linear(h, Wk, bk, scale_k)
        qm = jnp.concatenate([-q[:, :1], q[:, 1:]], axis=-1)
        att = 2.0 + 2.0 * (qm @ k.T)
        att = jax.nn.sigmoid(att / att_scale + att_bias)
        att = adj * att
        support = att @ h
        inner = -support[:, :1] ** 2 + jnp.sum(support[:, 1:] ** 2, axis=-1, keepdims=True)
        denorm = jnp.sqrt(jnp.clip(jnp.abs(-inner), 1e-08, None))
        return support / denorm

    def _L1_gnn_ref(X, adj, W, b):
        import jax, jax.numpy as jnp
        import numpy as np
        N, D_IN, D_OUT = (8192, 64, 64)
        AVG_DEG = 32.0
        L2_EPS = 1e-12
        deg = jnp.clip(jnp.sum(adj, axis=1, keepdims=True) + 1.0, 1.0, None)
        h_neigh = (adj @ X + X) / deg
        concat = jnp.concatenate([X, h_neigh], axis=1)
        z = concat @ W + b
        out = jax.nn.relu(z)
        norm = jnp.linalg.norm(out, axis=1, keepdims=True)
        return out / jnp.maximum(norm, L2_EPS)
    x = _layernorm(x + _L0_gnn_ref(x, adj, L0_gnn_W, L0_gnn_b, L0_gnn_scale, L0_gnn_Wq, L0_gnn_bq, L0_gnn_scale_q, L0_gnn_Wk, L0_gnn_bk, L0_gnn_scale_k, L0_gnn_att_bias, L0_gnn_att_scale), axis=-1)
    x = _layernorm(x + _L1_gnn_ref(x, adj, L1_gnn_W, L1_gnn_b), axis=-1)
    return x

_drawn_inputs = setup_inputs


def setup_inputs(seed=0):
    import zlib

    import numpy as np

    out = dict(_drawn_inputs(seed))
    spreads = {'L0_gnn_b': (0.0, 0.1), 'L0_gnn_bq': (0.0, 2.0), 'L0_gnn_bk': (0.0, 2.0)}
    factors = {'L0_gnn_Wq': 103.611, 'L0_gnn_Wk': 21.352, 'L1_gnn_b': 3.896}
    for name, (base, spread) in spreads.items():
        noise = np.random.default_rng([zlib.crc32(name.encode()), seed]).standard_normal(out[name].shape)
        drawn = base * np.exp(spread * noise) if base else spread * noise
        out[name] = jnp.asarray(drawn.astype(out[name].dtype))
    for name, factor in factors.items():
        out[name] = (out[name] * factor).astype(out[name].dtype)
    return out
```

```python
from contextlib import ExitStack

import concourse.bass as bass
from concourse import mybir

F32 = mybir.dt.float32
F16 = mybir.dt.float16
ALU = mybir.AluOpType
ACT = mybir.ActivationFunctionType
AX = mybir.AxisListType

P = 128
N = 8192
D = 64
NT = N // P
S = 512
NB = N // S
T = S // P
STEPS_A = NB * NB
STEPS_B = NB * (NB + 1) // 2
RING = 8
AHEAD = 3
CH = 8
NCH = NT // CH
FULL = 32768.0
EPS = 1e-5
(ES, ESQ, ESK, ATT_BIAS, ATT_SCALE) = range(5)


def two_layers(nc, adj_sq, x_nat, x_t, w_t, wqk_t, w1, b1, scalars, out):
    ctx = ExitStack()
    with ctx:
        def sb(name, shape, dt=F32):
            return ctx.enter_context(nc.sbuf_tensor(name, shape, dt))

        def sem(name):
            return ctx.enter_context(nc.semaphore(name))

        def pb(name, shape, dt=F32):
            return ctx.enter_context(nc.psum_tensor(name, shape, dt))

        kst = sb("k_stack", [P, N], F16)
        q1 = sb("q_stack", [P, N], F16)
        q2 = sb("q_stack_swapped", [P, N], F16)
        h = sb("h", [P, NT, D])
        xn = sb("x_then_x1", [P, NT, D])
        nb_a = sb("neighbour_sum_a", [P, NT, D])
        deg_a = sb("degree_a", [P, NT])
        ident = sb("ident", [P, P])
        ident16 = sb("ident16", [P, P], F16)
        fold = sb("fold", [P, D])
        ones = sb("ones", [P, P])
        zero16 = sb("zero16", [P, S], F16)
        w1_sb = sb("w1_sb", [P, D])
        b1_sb = sb("b1_sb", [1, D])
        sc_in = sb("scalars_sb", [P, 5])
        ex = sb("exp_scales", [P, 4])
        cst = sb("score_constants", [P, 8])
        half = sb("minus_half", [P, 32])
        minus_one = sb("minus_one", [P, T])
        phalf = sb("plus_half", [P, 32])

        bank = [pb(f"bank{i}", [P, 512]) for i in range(8)]
        sc = bank[0:4]
        acc_sup, acc_nb, acc_deg, misc = bank[4:8]

        names = """loaded consts_ready ones_ready
            lin_h_ready sig_h_ready ratio_h_ready factor_h_ready h_ready h_t_ready h_rows_ready
            lin_qk_ready sig_qk_ready ratio_qk_ready factor_qk_ready qk_ready hi_ready lo_ready
            stack_t_ready stacks_a stacks_v prologue_chain setup_chain exps_ready score_consts_ready
            adj_landed values_ready chunk_used0 chunk_used1 att_ready0 att_ready1 prod_ready0 prod_ready1
            sup_t_ready sup_nat_ready sup_saved nb_t_ready deg_s_ready nb_nat_ready nb_saved
            x1_ready deg_chain pool_chain pool_b_chain b_used0 b_used1 b_static0 b_static1 deg_counted
            b_nb_t_ready b_deg_s_ready b_nat_ready b_rows_ready cat_ready cat_t_psum cat_t_ready z_ready
            relu_ready b_chain out_ready out_stored nb_a_zero""".split()
        m = {n: sem(n) for n in names}
        scores_ready = [sem(f"scores_ready{t}") for t in range(T)]
        slot_landed = [sem(f"slot_landed{r}") for r in range(RING)]
        chunk_used = [m["chunk_used0"], m["chunk_used1"]]
        att_ready = [m["att_ready0"], m["att_ready1"]]
        prod_ready = [m["prod_ready0"], m["prod_ready1"]]
        b_used = [m["b_used0"], m["b_used1"]]
        b_static = [m["b_static0"], m["b_static1"]]

        with ExitStack() as pro:
            def tmp(name, shape, dt=F32):
                return pro.enter_context(nc.sbuf_tensor(name, shape, dt))

            xt = tmp("x_t_sb", [D + 1, N])
            w_sb = tmp("w_sb", [D + 1, D])
            wqk_sb = tmp("wqk_sb", [D + 1, 2 * D])
            ht = [tmp(f"h_t{i}", [D + 1, CH * P]) for i in range(2)]
            sqh = tmp("sq_h", [P, CH, D])
            sqqk = tmp("sq_qk", [P, 2 * CH, D])
            sigh = tmp("sig_h", [P, CH])
            sigqk = tmp("sig_qk", [P, CH, 2])
            th = tmp("time_h", [P, CH])
            vh = tmp("ratio_h", [P, CH])
            uh = tmp("num_h", [P, CH])
            fh = tmp("factor_h", [P, CH])
            tqk = tmp("time_qk", [P, CH, 2])
            vqk = tmp("ratio_qk", [P, CH, 2])
            uqk = tmp("num_qk", [P, CH, 2])
            fqk = tmp("factor_qk", [P, CH, 2])
            gqk = tmp("scaled_factor_qk", [P, CH, 2])
            e2 = tmp("exp_pair", [P, CH, 2])
            c2 = tmp("scale_pair", [P, CH, 2])
            c2s = tmp("signed_scale_pair", [P, CH, 2])
            qk32 = [tmp(f"qk32_{i}", [P, CH, 2, D]) for i in range(2)]
            natq = [tmp(f"nat_q{i}", [P, CH, 3, D], F16) for i in range(2)]
            natk = [tmp(f"nat_k{i}", [P, CH, 2, D], F16) for i in range(2)]

            lin_h = bank[0][:, :].rearrange("p (t d) -> p t d", d=D)
            hT = [bank[1], bank[2]]
            lin_qk = [bank[3][:, :].rearrange("p (t c d) -> p t c d", c=2, d=D),
                      bank[4][:, :].rearrange("p (t c d) -> p t c d", c=2, d=D)]
            stk, st1, st2 = (bank[i][:, :].bitcast(F16) for i in (5, 6, 7))

            def pow_into(pool, out_, base, exponent):
                return pool.tensor_tensor(out_, base, exponent, ALU.pow)

            with nc.Block() as block:
                @block.sync
                def _(sp):
                    for dst, src in ((sc_in[:, :], scalars), (w_sb[:, :], w_t), (wqk_sb[:, :], wqk_t),
                                     (xt[0:D, :], x_t), (xn[:, :, :], x_nat), (w1_sb[:, :], w1),
                                     (b1_sb[:, :], b1)):
                        sp.dma_start(dst, src).then_inc(m["loaded"], 16)

                @block.gpsimd
                def _(pool):
                    chain = m["pool_chain"]
                    pool.memset(xt[D:D + 1, :], 1.0).then_inc(m["ones_ready"], 1)
                    pool.drain()
                    for b in range(2):
                        pool.memset(ht[b][D:D + 1, :], 1.0).then_inc(m["ones_ready"], 1)
                        pool.drain()
                    pool.memset(half[:, :], -0.5).then_inc(m["ones_ready"], 1)
                    pool.memset(phalf[:, :], 0.5).then_inc(m["ones_ready"], 1)
                    pool.memset(minus_one[:, :], -1.0).then_inc(m["ones_ready"], 1)
                    pool.memset(ident[:, :], 0.0).then_inc(chain, 1)
                    pool.wait_ge(chain, 1)
                    pool.affine_select(out=ident[:, :], in_=ident[:, :], compare_op=ALU.not_equal, fill=1.0,
                                       base=0, pattern=[[-1, P]], channel_multiplier=1).then_inc(chain, 1)
                    pool.wait_ge(chain, 2)
                    pool.tensor_copy(ident16[:, :], ident[:, :]).then_inc(m["ones_ready"], 1)
                    pool.memset(ones[:, :], 1.0).then_inc(m["ones_ready"], 1)
                    pool.memset(zero16[:, :], 0.0).then_inc(m["ones_ready"], 1)
                    pool.memset(fold[:, :], 0.0).then_inc(chain, 1)
                    pool.wait_ge(chain, 3)
                    pool.affine_select(out=fold[:, :], in_=fold[:, :], compare_op=ALU.not_equal, fill=1.0,
                                       base=0, pattern=[[-1, D]], channel_multiplier=1).then_inc(chain, 1)
                    pool.wait_ge(chain, 4)
                    pool.affine_select(out=fold[:, :], in_=fold[:, :], compare_op=ALU.not_equal, fill=1.0,
                                       base=-D, pattern=[[-1, D]], channel_multiplier=1)\
                        .then_inc(m["ones_ready"], 1)
                    pool.memset(nb_a[:, 0:T, :], 0.0).then_inc(m["nb_a_zero"], 1)
                    pool.memset(deg_a[:, 0:T], 0.0).then_inc(m["nb_a_zero"], 1)
                    for n in range(NCH + 1):
                        if n < NCH:
                            pool.wait_ge(m["ratio_h_ready"], n + 1)
                            if n >= 1:
                                pool.wait_ge(m["h_ready"], n)
                            pow_into(pool, fh[:, :], vh[:, :], phalf[:, 0:CH]).then_inc(m["factor_h_ready"], 1)
                        if n >= 1:
                            pool.wait_ge(m["ratio_qk_ready"], n)
                            if n >= 2:
                                pool.wait_ge(m["qk_ready"], n - 1)
                            pow_into(pool, fqk[:, :, :], vqk[:, :, :],
                                     phalf[:, 0:2 * CH].rearrange("p (t c) -> p t c", c=2))\
                                .then_inc(m["factor_qk_ready"], 1)

                @block.tensor
                def _(pe):
                    pe.wait_ge(m["loaded"], 16 * 7)
                    pe.wait_ge(m["ones_ready"], 10)
                    for n in range(NCH + 2):
                        if n < NCH:
                            if n >= 1:
                                pe.wait_ge(m["h_ready"], n)
                            for t in range(CH):
                                c = (n * CH + t) * P
                                mm = pe.matmul(lin_h[:, t, :], xt[:, c:c + P], w_sb[:, :], start=True, stop=True)
                            mm.then_inc(m["lin_h_ready"], 1)
                        if 1 <= n <= NCH:
                            k = n - 1
                            pe.wait_ge(m["h_ready"], k + 1)
                            if k >= 1:
                                pe.wait_ge(m["h_rows_ready"], k)
                            for t in range(CH):
                                mm = pe.transpose(hT[t // 4][0:D, (t % 4) * P:(t % 4 + 1) * P],
                                                  h[:, k * CH + t, :], ident[:, :])
                            mm.then_inc(m["h_t_ready"], 1)
                            pe.wait_ge(m["h_rows_ready"], k + 1)
                            if k >= 1:
                                pe.wait_ge(m["qk_ready"], k)
                            for t in range(CH):
                                mm = pe.matmul(bank[3 + t // 4][:, (t % 4) * P:(t % 4 + 1) * P],
                                               ht[k % 2][:, t * P:(t + 1) * P], wqk_sb[:, :],
                                               start=True, stop=True)
                            mm.then_inc(m["lin_qk_ready"], 1)
                        if n >= 2:
                            k = n - 2
                            pe.wait_ge(m["hi_ready"], k + 1)
                            pe.wait_ge(m["lo_ready"], k + 1)
                            if k >= 1:
                                pe.wait_ge(m["stacks_a"], k)
                                pe.wait_ge(m["stacks_v"], k)
                            for t in range(CH):
                                o = slice(t * P, (t + 1) * P)
                                pe.transpose(stk[:, o], natk[k % 2][:, t, :, :].rearrange("p c d -> p (c d)"),
                                             ident16[:, :])
                                pe.transpose(st1[:, o], natq[k % 2][:, t, 0:2, :].rearrange("p c d -> p (c d)"),
                                             ident16[:, :])
                                mm = pe.transpose(st2[:, o], natq[k % 2][:, t, 1:3, :]
                                                  .rearrange("p c d -> p (c d)"), ident16[:, :])
                            mm.then_inc(m["stack_t_ready"], 1)

                @block.scalar
                def _(act):
                    act.wait_ge(m["loaded"], 16 * 7)
                    act.activation(ex[:, 0:3], sc_in[:, ES:ESK + 1], ACT.Exp).then_inc(m["exps_ready"], 1)

                    for n in range(NCH + 2):
                        if n < NCH:
                            act.wait_ge(m["lin_h_ready"], n + 1)
                            if n >= 1:
                                act.wait_ge(m["ratio_h_ready"], n)
                            act.activation(sigh[:, :], lin_h[:, :, 0], ACT.Sigmoid)
                            act.activation(sqh[:, :, :], lin_h, ACT.Square).then_inc(m["sig_h_ready"], 1)
                        if 1 <= n <= NCH:
                            k = n - 1
                            act.wait_ge(m["h_t_ready"], k + 1)
                            if k >= 2:
                                act.wait_ge(m["lin_qk_ready"], k - 1)
                            for b in range(2):
                                mm = act.activation(ht[k % 2][0:D, b * 512:(b + 1) * 512], hT[b][0:D, :], ACT.Copy)
                            mm.then_inc(m["h_rows_ready"], 1)
                            act.wait_ge(m["lin_qk_ready"], k + 1)
                            if k >= 1:
                                act.wait_ge(m["ratio_qk_ready"], k)
                            for b in range(2):
                                act.activation(sigqk[:, 4 * b:4 * b + 4, :], lin_qk[b][:, :, :, 0], ACT.Sigmoid)
                                mm = act.activation(sqqk[:, CH * b:CH * b + CH, :], bank[3 + b][:, :]
                                                    .rearrange("p (t d) -> p t d", d=D), ACT.Square)
                            mm.then_inc(m["sig_qk_ready"], 1)
                        if n >= 2:
                            k = n - 2
                            act.wait_ge(m["qk_ready"], k + 1)
                            if k >= 2:
                                act.wait_ge(m["stack_t_ready"], k - 1)
                            act.activation(natq[k % 2][:, :, 0, :], qk32[k % 2][:, :, 0, :], ACT.Copy)
                            act.activation(natk[k % 2][:, :, 0, :], qk32[k % 2][:, :, 1, :], ACT.Copy)
                            act.activation(natq[k % 2][:, :, 2, :], qk32[k % 2][:, :, 0, :], ACT.Copy)\
                                .then_inc(m["hi_ready"], 1)
                            act.wait_ge(m["stack_t_ready"], k + 1)
                            o = slice(k * CH * P, (k + 1) * CH * P)
                            act.activation(kst[:, o], stk, ACT.Copy)
                            act.activation(q1[:, o], st1, ACT.Copy).then_inc(m["stacks_a"], 1)

                @block.vector
                def _(dve):
                    chain = m["prologue_chain"]
                    done = [0]

                    def then(ins):
                        ins.then_inc(chain, 1)
                        done[0] += 1
                        dve.wait_ge(chain, done[0])

                    dve.wait_ge(m["exps_ready"], 1)
                    then(dve.tensor_scalar(cst[:, 0:2], ex[:, 1:3], 1.1, 1.0 / FULL, ALU.add, ALU.mult))
                    then(dve.reciprocal(cst[:, 2:4], cst[:, 0:2]))
                    then(dve.reciprocal(cst[:, 4:5], sc_in[:, ATT_SCALE:ATT_SCALE + 1]))
                    then(dve.tensor_scalar(cst[:, 5:6], cst[:, 4:5], 2.0, None, ALU.mult))
                    then(dve.tensor_tensor(cst[:, 6:7], cst[:, 5:6], sc_in[:, ATT_BIAS:ATT_BIAS + 1], ALU.add))
                    then(dve.tensor_scalar(cst[:, 5:6], cst[:, 5:6], cst[:, 0:1], cst[:, 1:2], ALU.mult, ALU.mult))
                    for c in range(2):
                        then(dve.memset(e2[:, :, c], 1.0))
                        then(dve.memset(c2[:, :, c], 1.0))
                        then(dve.tensor_scalar(c2s[:, :, c], c2[:, :, c], cst[:, 2 + c:3 + c],
                                               (-1.0, 1.0)[c], ALU.mult, ALU.mult))
                        then(dve.tensor_scalar(c2[:, :, c], c2[:, :, c], cst[:, 2 + c:3 + c], None, ALU.mult))
                        then(dve.tensor_scalar(e2[:, :, c], e2[:, :, c], ex[:, 1 + c:2 + c], None, ALU.mult))

                    for n in range(NCH + 2):
                        if n < NCH:
                            dve.wait_ge(m["sig_h_ready"], n + 1)
                            if n >= 1:
                                dve.wait_ge(m["factor_h_ready"], n)
                            dve.tensor_scalar(th[:, :], sigh[:, :], ex[:, 0:1], 1.1, ALU.mult, ALU.add)
                            then(dve.tensor_reduce(uh[:, :], sqh[:, :, 1:D], AX.X, ALU.add))
                            then(dve.tensor_scalar(uh[:, :], uh[:, :], 1e-8, None, ALU.max))
                            dve.reciprocal(uh[:, :], uh[:, :])
                            then(dve.tensor_tensor(vh[:, :], th[:, :], th[:, :], ALU.mult))
                            dve.scalar_tensor_tensor(out=vh[:, :], in0=vh[:, :], scalar=-1.0, in1=uh[:, :],
                                                     op0=ALU.add, op1=ALU.mult).then_inc(m["ratio_h_ready"], 1)
                        if 1 <= n <= NCH:
                            k = n - 1
                            dve.wait_ge(m["sig_qk_ready"], k + 1)
                            if k >= 1:
                                dve.wait_ge(m["factor_qk_ready"], k)
                            v3 = "p (t c) -> p t c"
                            then(dve.tensor_tensor(tqk[:, :, :], sigqk[:, :, :], e2[:, :, :], ALU.mult))
                            then(dve.tensor_scalar(tqk[:, :, :], tqk[:, :, :], 1.1, None, ALU.add))
                            then(dve.tensor_reduce(uqk[:, :, :].rearrange("p t c -> p (t c)"),
                                                   sqqk[:, :, 1:D], AX.X, ALU.add))
                            then(dve.tensor_scalar(uqk[:, :, :], uqk[:, :, :], 1e-8, None, ALU.max))
                            dve.reciprocal(uqk[:, :, :], uqk[:, :, :])
                            then(dve.tensor_tensor(vqk[:, :, :], tqk[:, :, :], tqk[:, :, :], ALU.mult))
                            dve.scalar_tensor_tensor(out=vqk[:, :, :], in0=vqk[:, :, :], scalar=-1.0,
                                                     in1=uqk[:, :, :], op0=ALU.add, op1=ALU.mult)\
                                .then_inc(m["ratio_qk_ready"], 1)
                        if n < NCH:
                            dve.wait_ge(m["factor_h_ready"], n + 1)
                            dve.tensor_tensor(h[:, n * CH:(n + 1) * CH, 1:D], lin_h[:, :, 1:D],
                                              fh[:, :].unsqueeze(2).to_broadcast([P, CH, D - 1]), ALU.mult)
                            dve.tensor_copy(h[:, n * CH:(n + 1) * CH, 0], th[:, :]).then_inc(m["h_ready"], 1)
                        if n >= 2:
                            k = n - 2
                            dve.wait_ge(m["hi_ready"], k + 1)
                            dve.tensor_tensor(natq[k % 2][:, :, 1, :], qk32[k % 2][:, :, 0, :],
                                              natq[k % 2][:, :, 0, :], ALU.subtract)
                            dve.tensor_tensor(natk[k % 2][:, :, 1, :], qk32[k % 2][:, :, 1, :],
                                              natk[k % 2][:, :, 0, :], ALU.subtract).then_inc(m["lo_ready"], 1)
                            dve.wait_ge(m["stack_t_ready"], k + 1)
                            dve.tensor_copy(q2[:, k * CH * P:(k + 1) * CH * P], st2).then_inc(m["stacks_v"], 1)
                        if 1 <= n <= NCH:
                            k = n - 1
                            dve.wait_ge(m["factor_qk_ready"], k + 1)
                            if k >= 2:
                                dve.wait_ge(m["hi_ready"], k - 1)
                            then(dve.tensor_tensor(gqk[:, :, :], fqk[:, :, :], c2[:, :, :], ALU.mult))
                            for b in range(2):
                                dve.tensor_tensor(qk32[k % 2][:, 4 * b:4 * b + 4, :, 1:D], lin_qk[b][:, :, :, 1:D],
                                                  gqk[:, 4 * b:4 * b + 4, :].unsqueeze(3)
                                                  .to_broadcast([P, 4, 2, D - 1]), ALU.mult)
                            dve.tensor_tensor(qk32[k % 2][:, :, :, 0], tqk[:, :, :], c2s[:, :, :], ALU.mult)\
                                .then_inc(m["qk_ready"], 1)

        ring = sb("adjacency_ring", [P, RING, T, S])
        prod = [sb(f"product{u}", [P, 2, S]) for u in range(2)]
        hs = sb("h_of_step", [P, T, D])
        xs = sb("x1_of_step", [P, T, D])
        sup_t = sb("support_t", [P, S])
        nb_t = sb("neighbour_t", [P, S])
        deg_s = sb("degree_s", [P, S])
        sup_n = sb("support_nat", [P, T, D])
        wa = sb("work_a", [P, T, D])
        wb = sb("work_b", [P, T, D])
        wc = sb("work_c", [P, T, D])
        rc = sb("row_scalars", [P, 8, T])
        cat = sb("cat", [P, T, 2 * D])
        cat_t = sb("cat_t", [P, T, P])
        relu = sb("relu", [P, T, D])
        y_out = [sb(f"y_out", [P, T, D])]
        nbn = sb("nb_total", [P, T, D])
        dgn = sb("deg_total", [P, 3, T])

        block = ctx.enter_context(nc.Block())

        def square(idx):
            return adj_sq[bass.ds(idx, 1), :, :].rearrange("s p f -> (s p) f")

        def slot(r):
            return ring[:, r, :, :].rearrange("p t i -> p (t i)")

        @block.sync
        def _(sp):
            def relay(k_slot, landed):
                sp.wait_ge(slot_landed[k_slot], landed)
                sp.sem_inc(m["adj_landed"], 1)

            for r in range(RING):
                sp.dma_start(slot(r), adj_sq[r]).then_inc(slot_landed[r], 16)
            for r in range(AHEAD):
                relay(r, 16)
            with sp.Fori(1, STEPS_A // RING) as g:
                for r in range(RING):
                    relay((r + AHEAD) % RING, (g + (r + AHEAD) // RING) * 16)
                    sp.wait_ge(chunk_used[1], (g - 1) * RING + r + 1)
                    sp.dma_start(slot(r), square(g * RING + r)).then_inc(slot_landed[r], 16)
            sq = sp.alloc_register("square")
            wrap = sp.alloc_register("wrap")
            jump = sp.alloc_register("jump")
            sp.reg_mov(sq, NB * NB - 1)

            def issue_b(r):
                sp.dma_start(slot(r), square(sp.snap(sq, min_val=0, max_val=NB * NB - 1)))\
                    .then_inc(slot_landed[r], 16)
                sp.reg_alu(sq, sq, 1, ALU.add)
                sp.reg_alu(wrap, sq, NB - 1, ALU.bitwise_and)
                sp.reg_alu(wrap, wrap, NB - 1, ALU.add)
                sp.reg_alu(wrap, wrap, 4, ALU.logical_shift_right)
                sp.reg_alu(wrap, wrap, 1, ALU.bitwise_xor)
                sp.reg_alu(jump, sq, 4, ALU.logical_shift_right)
                sp.reg_alu(jump, jump, NB + 1, ALU.mult)
                sp.reg_alu(jump, jump, 2 * (NB + 1), ALU.subtract)
                sp.reg_alu(jump, jump, sq, ALU.subtract)
                sp.reg_alu(jump, jump, wrap, ALU.mult)
                sp.reg_alu(sq, sq, jump, ALU.add)

            ga = STEPS_A // RING
            for r in range(RING):
                relay((r + AHEAD) % RING, 16 * (ga + (r + AHEAD) // RING))
                sp.wait_ge(chunk_used[1], (ga - 1) * RING + r + 1)
                issue_b(r)
            with sp.Fori(0, STEPS_B // RING - 1) as g:
                for r in range(RING):
                    relay((r + AHEAD) % RING, (g + (ga + 1) + (r + AHEAD) // RING) * 16)
                    sp.wait_ge(b_used[1], g * RING + r + 1)
                    sp.wait_ge(m["deg_counted"], g * RING + r + 1)
                    issue_b(r)
            for r in range(AHEAD, RING):
                relay(r, 16 * (STEPS_A + STEPS_B) // RING)

        @block.tensor
        def _(pe):
            def scores(s1, u):
                kcol = pe.snap((s1 & (NB - 1)) * S)
                qcol = pe.snap(((s1 >> 4) & (NB - 1)) * S)
                pe.wait_ge(prod_ready[u], s1)
                for t in (2 * u, 2 * u + 1):
                    w = kst[:, bass.ds(kcol + t * P, P)]
                    pe.matmul(sc[t][:, :], w, q1[:, bass.ds(qcol, S)], start=True, stop=False)
                    pe.matmul(sc[t][:, :], w, q2[:, bass.ds(qcol, S)], start=False, stop=True)\
                        .then_inc(scores_ready[t], 1)

            def add_to(acc, lhs, rhs):
                return pe.matmul(acc, lhs, rhs, start=False, stop=False, skip_group_check=True)

            def support(u, t, half_):
                return add_to(acc_sup[D * half_:D * half_ + D, :], hs[:, t, :], prod[u][:, t % 2, :])

            def zero(acc):
                pe.matmul(acc[:, :], zero16[:, 0:P], zero16[:, :], start=True, stop=False, skip_group_check=True)

            def upper(s1):
                for u in range(2):
                    scores(s1, u)
                    if u == 0:
                        pe.wait_ge(m["values_ready"], s1)
                    support(u, 2 * u, 0)
                    support(u, 2 * u + 1, 1).then_inc(chunk_used[u], 1)

            def lower(s1):
                sl = pe.snap((s1 - 1) & (RING - 1))
                for u in range(2):
                    scores(s1, u)
                    if u == 0:
                        pe.wait_ge(m["values_ready"], s1)
                    for t in (2 * u, 2 * u + 1):
                        add_to(acc_nb[0:D, :], xs[:, t, :],
                               ring[:, bass.ds(sl, 1), t, :].rearrange("p a i -> p (a i)"))
                        mm = support(u, t, 1)
                    mm.then_inc(chunk_used[u], 1)

            def end_block(I, has_lower):
                if has_lower:
                    pe.wait_ge(m["nb_t_ready"], I)
                    pe.wait_ge(m["deg_s_ready"], I)
                    for c in range(T):
                        o = slice(c * P, (c + 1) * P)
                        pe.matmul(acc_deg[:, c * D:(c + 1) * D], nb_t[0:D, o], fold[0:D, :], start=True, stop=True)
                        mm = pe.matmul(acc_deg[:, T * D + c:T * D + c + 1], deg_s[:, o], ones[:, 0:1],
                                       start=True, stop=True)
                    mm.then_inc(m["nb_nat_ready"], 1)
                pe.wait_ge(m["sup_t_ready"], I + 1)
                pe.wait_ge(m["sup_saved"], I)
                for c in range(T):
                    mm = pe.matmul(misc[:, c * D:(c + 1) * D], sup_t[:, c * P:(c + 1) * P], fold[:, :],
                                   start=True, stop=True)
                mm.then_inc(m["sup_nat_ready"], 1)
                zero(acc_sup)
                zero(acc_nb)

            zero(acc_sup)
            zero(acc_nb)
            for t in range(T):
                w = kst[:, t * P:(t + 1) * P]
                pe.matmul(sc[t][:, :], w, q1[:, 0:S], start=True, stop=False)
                pe.matmul(sc[t][:, :], w, q2[:, 0:S], start=False, stop=True).then_inc(scores_ready[t], 1)
            with pe.Fori(0, NB) as J:
                upper(pe.snap(J + 1))
            end_block(0, False)
            with pe.Fori(1, NB) as I:
                with pe.Fori(0, I) as J:
                    lower(pe.snap(NB * I + J + 1))
                with pe.Fori(I, NB) as J:
                    upper(pe.snap(NB * I + J + 1))
                end_block(I, True)

            with pe.Fori(0, NB) as K:
                with pe.Fori(0, K + 1) as J:
                    n = pe.snap((K * (K + 1) >> 1) + J)
                    sl = pe.snap(n & (RING - 1))
                    for u in range(2):
                        pe.wait_ge(b_static[u], n + 1)
                        add_to(acc_nb[0:D, :], xs[:, 2 * u, :],
                               ring[:, bass.ds(sl, 1), 2 * u, :].rearrange("p a i -> p (a i)"))
                        add_to(acc_nb[D:P, :], xs[:, 2 * u + 1, :], prod[u][:, 0, :]).then_inc(b_used[u], 1)
                pe.wait_ge(m["b_nb_t_ready"], K + 1)
                pe.wait_ge(m["b_deg_s_ready"], K + 1)
                for c in range(T):
                    o = slice(c * P, (c + 1) * P)
                    pe.matmul(acc_deg[:, c * D:(c + 1) * D], nb_t[:, o], fold[:, :], start=True, stop=True)
                    mm = pe.matmul(acc_deg[:, T * D + c:T * D + c + 1], deg_s[:, o], ones[:, 0:1],
                                   start=True, stop=True)
                mm.then_inc(m["b_nat_ready"], 1)
                zero(acc_nb)
                pe.wait_ge(m["cat_ready"], K + 1)
                pe.wait_ge(m["relu_ready"], K)
                for c in range(T):
                    mm = pe.transpose(misc[:, c * P:(c + 1) * P], cat[:, c, :], ident[:, :])
                mm.then_inc(m["cat_t_psum"], 1)
                pe.wait_ge(m["cat_t_ready"], K + 1)
                for c in range(T):
                    pe.matmul(misc[:, c * D:(c + 1) * D], cat_t[:, c, :], w1_sb[:, :], start=True, stop=False)
                    mm = pe.matmul(misc[:, c * D:(c + 1) * D], ones[0:1, :], b1_sb[:, :], start=False, stop=True)
                mm.then_inc(m["z_ready"], 1)

        @block.scalar
        def _(act):
            def sigmoids(s1):
                for t in range(T):
                    act.wait_ge(scores_ready[t], s1 + 1)
                    ins = act.activation(sc[t][:, :], sc[t][:, :], ACT.Sigmoid, bias=cst[:, 6:7],
                                         scale=cst[:, 5:6])
                    if t % 2:
                        ins.then_inc(att_ready[t // 2], 1)

            def values(s, J, with_x1):
                act.wait_ge(chunk_used[1], s)
                if with_x1:
                    act.wait_ge(m["x1_ready"], J + 1)
                    act.activation(xs[:, :, :], xn[:, bass.ds(J * T, T), :], ACT.Copy)
                act.activation(hs[:, :, :], h[:, bass.ds(J * T, T), :], ACT.Copy).then_inc(m["values_ready"], 1)

            def end_block(I, has_lower):
                act.wait_ge(chunk_used[1], (I + 1) * NB)
                act.activation(sup_t[:, :], acc_sup[:, :], ACT.Copy).then_inc(m["sup_t_ready"], 1)
                if has_lower:
                    act.wait_ge(m["nb_nat_ready"], I)
                    act.activation(nb_a[:, bass.ds(I * T, T), :],
                                   acc_deg[:, 0:T * D].rearrange("p (t d) -> p t d", d=D), ACT.Copy)
                    act.activation(deg_a[:, bass.ds(I * T, T)], acc_deg[:, T * D:T * D + T], ACT.Copy)\
                        .then_inc(m["nb_saved"], 1)
                act.wait_ge(m["sup_nat_ready"], I + 1)
                act.wait_ge(m["x1_ready"], I)
                act.activation(sup_n[:, :, :], misc[:, 0:T * D].rearrange("p (t d) -> p t d", d=D), ACT.Copy)\
                    .then_inc(m["sup_saved"], 1)

            sigmoids(0)
            with act.Fori(0, NB) as J:
                values(J, J, False)
                sigmoids(act.snap(J + 1))
            end_block(0, False)
            with act.Fori(1, NB) as I:
                with act.Fori(0, I) as J:
                    s = act.snap(NB * I + J)
                    values(s, J, True)
                    sigmoids(s + 1)
                act.wait_ge(chunk_used[1], I * NB + I)
                act.wait_ge(m["nb_nat_ready"], I - 1)
                act.activation(nb_t[0:D, :], acc_nb[0:D, :], ACT.Copy).then_inc(m["nb_t_ready"], 1)
                with act.Fori(I, NB) as J:
                    s = act.snap(NB * I + J)
                    values(s, J, False)
                    sigmoids(s + 1)
                end_block(I, True)

            with act.Fori(0, NB) as K:
                I = act.snap((K * (NB - 1) + (NB - 1)) & (NB - 1))
                with act.Fori(0, K + 1) as d:
                    n = act.snap((K * (K + 1) >> 1) + d)
                    sl = act.snap(n & (RING - 1))
                    J = act.snap((I + d) & (NB - 1))
                    jt = act.snap(J * T)
                    act.wait_ge(m["adj_landed"], n + (STEPS_A + 1))
                    act.wait_ge(m["x1_ready"], J + 1)
                    for u in range(2):
                        act.wait_ge(b_used[u], n)
                        act.activation(xs[:, 2 * u:2 * u + 2, :], xn[:, bass.ds(jt + 2 * u, 2), :], ACT.Copy)
                        act.activation(prod[u][:, 0, :],
                                       ring[:, bass.ds(sl, 1), 2 * u + 1, :].rearrange("p a i -> p (a i)"),
                                       ACT.Copy).then_inc(b_static[u], 1)
                act.wait_ge(b_used[1], ((K + 1) * (K + 2)) >> 1)
                act.activation(nb_t[:, :], acc_nb[:, :], ACT.Copy).then_inc(m["b_nb_t_ready"], 1)
                act.wait_ge(m["cat_t_psum"], K + 1)
                act.activation(cat_t[:, :, :], misc[:, :].rearrange("p (t i) -> p t i", t=T), ACT.Copy)\
                    .then_inc(m["cat_t_ready"], 1)
                act.wait_ge(m["z_ready"], K + 1)
                act.wait_ge(m["out_ready"], K)
                act.activation(relu[:, :, :], misc[:, 0:T * D].rearrange("p (t d) -> p t d", d=D), ACT.Relu)\
                    .then_inc(m["relu_ready"], 1)

        @block.vector
        def _(dve):
            chain = m["deg_chain"]

            def deg_add(sl, t, links):
                dve.wait_ge(chain, links)
                dve.tensor_tensor(acc_deg[:, :], acc_deg[:, :],
                                  ring[:, bass.ds(sl, 1), t, :].rearrange("p a i -> p (a i)"), ALU.add)\
                    .then_inc(chain, 1)

            def product(s, sl, u):
                dve.wait_ge(att_ready[u], s + 1)
                dve.wait_ge(chunk_used[u], s)
                for t in range(2):
                    ins = dve.tensor_tensor(prod[u][:, t, :], sc[2 * u + t][:, :],
                                            ring[:, bass.ds(sl, 1), 2 * u + t, :].rearrange("p a i -> p (a i)"),
                                            ALU.mult)
                ins.then_inc(prod_ready[u], 1)

            def upper(s):
                sl = dve.snap(s & (RING - 1))
                dve.wait_ge(m["adj_landed"], s + 1)
                for u in range(2):
                    product(s, sl, u)

            with dve.Fori(0, NB) as J:
                upper(J)
            with dve.Fori(1, NB) as I:
                dve.wait_ge(m["nb_saved"], I - 1)
                dve.memset(acc_deg[:, :], 0.0).then_inc(chain, 1)
                with dve.Fori(0, I) as J:
                    s = dve.snap(NB * I + J)
                    links = dve.snap(I + 2 * (I - 1) * I + 4 * J)
                    sl = dve.snap(s & (RING - 1))
                    dve.wait_ge(m["adj_landed"], s + 1)
                    for u in range(2):
                        for t in range(2):
                            deg_add(sl, 2 * u + t, links + (2 * u + t))
                        product(s, sl, u)
                dve.wait_ge(chain, I + 2 * (I + 1) * I)
                dve.tensor_copy(deg_s[:, :], acc_deg[:, :]).then_inc(m["deg_s_ready"], 1)
                with dve.Fori(I, NB) as J:
                    upper(dve.snap(NB * I + J))

            links_a = (NB - 1) + 2 * NB * (NB - 1)
            with dve.Fori(0, NB) as K:
                I = dve.snap((K * (NB - 1) + (NB - 1)) & (NB - 1))
                tiles = dve.snap(I * T)
                dve.wait_ge(m["nb_saved"], NB - 1)
                dve.memset(acc_deg[:, :], 0.0).then_inc(chain, 1)
                with dve.Fori(0, K + 1) as J:
                    n = dve.snap((K * (K + 1) >> 1) + J)
                    sl = dve.snap(n & (RING - 1))
                    links = dve.snap(links_a + 1 + K + 4 * n)
                    dve.wait_ge(m["adj_landed"], n + (STEPS_A + 1))
                    for t in range(T):
                        dve.wait_ge(chain, links + t)
                        ins = dve.tensor_tensor(acc_deg[:, :], acc_deg[:, :],
                                                ring[:, bass.ds(sl, 1), t, :].rearrange("p a i -> p (a i)"),
                                                ALU.add)
                        ins.then_inc(chain, 1)
                    dve.wait_ge(chain, links + 4)
                    dve.sem_inc(m["deg_counted"], 1)
                dve.tensor_copy(deg_s[:, :], acc_deg[:, :]).then_inc(m["b_deg_s_ready"], 1)

                b = m["b_chain"]
                at = dve.snap(K * 5)
                dve.wait_ge(m["b_nat_ready"], K + 1)
                dve.wait_ge(m["cat_t_psum"], K)
                dve.tensor_tensor(dgn[:, 0, :], acc_deg[:, T * D:T * D + T], deg_a[:, bass.ds(tiles, T)], ALU.add)\
                    .then_inc(b, 1)
                dve.tensor_tensor(nbn[:, :, :], acc_deg[:, 0:T * D].rearrange("p (t d) -> p t d", d=D),
                                  nb_a[:, bass.ds(tiles, T), :], ALU.add).then_inc(b, 1)
                dve.tensor_copy(cat[:, :, 0:D], xn[:, bass.ds(tiles, T), :])
                dve.wait_ge(b, at + 2)
                dve.tensor_scalar(dgn[:, 1, :], dgn[:, 0, :], 1.0, 1.0, ALU.add, ALU.max).then_inc(b, 1)
                dve.tensor_tensor(nbn[:, :, :], nbn[:, :, :], xn[:, bass.ds(tiles, T), :], ALU.add).then_inc(b, 1)
                dve.wait_ge(b, at + 4)
                dve.reciprocal(dgn[:, 2, :], dgn[:, 1, :]).then_inc(b, 1)
                dve.wait_ge(b, at + 5)
                dve.tensor_tensor(cat[:, :, D:2 * D], nbn[:, :, :],
                                  dgn[:, 2, :].unsqueeze(2).to_broadcast([P, T, D]), ALU.mult)\
                    .then_inc(m["cat_ready"], 1)

        @block.gpsimd
        def _(pool):
            def then(ins):
                pool.drain()

            def row(i):
                return rc[:, i, :]

            def spread(i):
                return rc[:, i, :].unsqueeze(2).to_broadcast([P, T, D])

            def row_sum(buf, out_row):
                w = D // 2
                while w >= 1:
                    dst = buf[:, :, 0:w] if w > 1 else row(out_row).unsqueeze(2)
                    then(pool.tensor_tensor(dst, buf[:, :, 0:w], buf[:, :, w:2 * w], ALU.add))
                    w //= 2

            def layernorm(src, last_out):
                then(pool.tensor_scalar(wb[:, :, :], src, 1.0, None, ALU.mult))
                row_sum(wb, 0)
                then(pool.tensor_scalar(row(1), row(0), 1.0 / D, None, ALU.mult))
                then(pool.tensor_tensor(wc[:, :, :], src, spread(1), ALU.subtract))
                then(pool.tensor_tensor(wb[:, :, :], wc[:, :, :], wc[:, :, :], ALU.mult))
                row_sum(wb, 2)
                then(pool.tensor_scalar(row(3), row(2), 1.0 / D, EPS, ALU.mult, ALU.add))
                then(pool.tensor_tensor(row(4), row(3), half[:, 0:T], ALU.pow))
                return pool.tensor_tensor(last_out, wc[:, :, :], spread(4), ALU.mult)

            with pool.Fori(0, NB) as I:
                x_blk = xn[:, bass.ds(I * T, T), :]
                pool.wait_ge(m["sup_saved"], I + 1)
                then(pool.tensor_tensor(wa[:, :, :], sup_n[:, :, :], sup_n[:, :, :], ALU.mult))
                then(pool.tensor_scalar(row(5), wa[:, :, 0], -2.0, None, ALU.mult))
                row_sum(wa, 6)
                then(pool.tensor_tensor(row(5), row(5), row(6), ALU.add))
                then(pool.tensor_scalar(row(6), row(5), 0.0, None, ALU.max))
                then(pool.tensor_scalar(row(7), row(5), 0.0, None, ALU.min))
                then(pool.tensor_tensor(row(6), row(6), row(7), ALU.subtract))
                then(pool.tensor_scalar(row(6), row(6), 1e-8, None, ALU.max))
                then(pool.tensor_tensor(row(5), row(6), half[:, 0:T], ALU.pow))
                then(pool.tensor_tensor(wa[:, :, :], sup_n[:, :, :], spread(5), ALU.mult))
                then(pool.tensor_tensor(wa[:, :, :], wa[:, :, :], x_blk, ALU.add))
                ins = layernorm(wa[:, :, :], x_blk)
                ins.then_inc(m["x1_ready"], 1)

            with pool.Fori(0, NB) as K:
                I = pool.snap((K * (NB - 1) + (NB - 1)) & (NB - 1))
                pool.wait_ge(m["out_stored"], K * 16)
                pool.wait_ge(m["relu_ready"], K + 1)
                then(pool.tensor_tensor(wa[:, :, :], relu[:, :, :], relu[:, :, :], ALU.mult))
                row_sum(wa, 5)
                then(pool.tensor_tensor(row(6), row(5), phalf[:, 0:T], ALU.pow))
                then(pool.tensor_scalar(row(6), row(6), 1e-12, None, ALU.max))
                then(pool.tensor_tensor(row(7), row(6), minus_one[:, :], ALU.pow))
                then(pool.tensor_tensor(wa[:, :, :], relu[:, :, :], spread(7), ALU.mult))
                then(pool.tensor_tensor(wa[:, :, :], wa[:, :, :], xn[:, bass.ds(I * T, T), :], ALU.add))
                ins = layernorm(wa[:, :, :], y_out[0][:, :, :])
                ins.then_inc(m["out_ready"], 1)
                pool.drain()
                pool.dma_start(out[bass.ds(I, 1), :, :].rearrange("s p f -> (s p) f"),
                               y_out[0][:, :, :].rearrange("p t d -> p (t d)")).then_inc(m["out_stored"], 16)
            pool.wait_ge(m["out_stored"], NB * 16)


def kernel(x, adj, L0_gnn_W, L0_gnn_b, L0_gnn_scale, L0_gnn_Wq, L0_gnn_bq, L0_gnn_scale_q, L0_gnn_Wk, L0_gnn_bk,
           L0_gnn_scale_k, L0_gnn_att_bias, L0_gnn_att_scale, L1_gnn_W, L1_gnn_b):
    import numpy as np
    import concourse.bacc as bacc
    from concourse.bass_utils import run_bass_kernel_spmd

    nc = bacc.Bacc("TRN2", target_bir_lowering=False, num_devices=1)
    x = np.asarray(x)
    scalars = np.stack([np.asarray(v).reshape(()) for v in
                        (L0_gnn_scale, L0_gnn_scale_q, L0_gnn_scale_k, L0_gnn_att_bias, L0_gnn_att_scale)])
    arrays = {
        "adj_sq": np.ascontiguousarray(np.asarray(adj).reshape(NB, S, NB, T, P).transpose(0, 2, 4, 3, 1))
        .reshape(NB * NB, P, T * S),
        "x_nat": np.ascontiguousarray(x.reshape(NT, P, D).transpose(1, 0, 2)),
        "x_t": np.ascontiguousarray(x.T),
        "w_t": np.concatenate([np.asarray(L0_gnn_W).T, np.asarray(L0_gnn_b)[None]]),
        "wqk_t": np.concatenate([np.concatenate([np.asarray(L0_gnn_Wq).T, np.asarray(L0_gnn_Wk).T], 1),
                                 np.concatenate([np.asarray(L0_gnn_bq), np.asarray(L0_gnn_bk)])[None]]),
        "w1": np.ascontiguousarray(np.asarray(L1_gnn_W)),
        "b1": np.ascontiguousarray(np.asarray(L1_gnn_b).reshape(1, D)),
        "scalars": np.ascontiguousarray(np.broadcast_to(scalars[None], (P, 5))),
    }
    args = [nc.dram_tensor(n, a.shape, F32, kind="ExternalInput").ap() for n, a in arrays.items()]
    out = nc.dram_tensor("x2", (NB, P, T * D), F32, kind="ExternalOutput").ap()
    two_layers(nc, *args, out)
    got = run_bass_kernel_spmd(nc, [arrays], core_ids=[0]).results[0]["x2"]
    return np.ascontiguousarray(np.asarray(got).reshape(NB, P, T, D).transpose(0, 2, 1, 3)).reshape(N, D)
```

```python
from contextlib import ExitStack

import concourse.bass as bass
from concourse import mybir

F32 = mybir.dt.float32
F16 = mybir.dt.float16
ALU = mybir.AluOpType
ACT = mybir.ActivationFunctionType
AX = mybir.AxisListType

P = 128
N = 8192
D = 64
NT = N // P
S = 512
NB = N // S
T = S // P
STEPS_A = NB * NB
STEPS_B = NB * (NB + 1) // 2
DSLOTS = 4
LOWER = NB * (NB - 1) // 2
RING = 8
AHEAD = 3
CH = 8
NCH = NT // CH
FULL = 32768.0
EPS = 1e-5
(ES, ESQ, ESK, ATT_BIAS, ATT_SCALE) = range(5)


def two_layers(nc, adj_sq, x_nat, x_t, w_t, wqk_t, w1, b1, scalars, out):
    ctx = ExitStack()
    with ctx:
        def sb(name, shape, dt=F32):
            return ctx.enter_context(nc.sbuf_tensor(name, shape, dt))

        def sem(name):
            return ctx.enter_context(nc.semaphore(name))

        def pb(name, shape, dt=F32):
            return ctx.enter_context(nc.psum_tensor(name, shape, dt))

        kst = sb("k_stack", [P, N], F16)
        q1 = sb("q_stack", [P, N], F16)
        q2 = sb("q_stack_swapped", [P, N], F16)
        h = sb("h", [P, NT, D])
        xn = sb("x_then_x1", [P, NT, D])
        nb_a = sb("neighbour_sum_a", [P, NT, D])
        deg_a = sb("degree_a", [P, NT])
        ident = sb("ident", [P, P])
        ident16 = sb("ident16", [P, P], F16)
        fold = sb("fold", [P, D])
        ones = sb("ones", [P, P])
        zero16 = sb("zero16", [P, S], F16)
        w1_sb = sb("w1_sb", [P, D])
        b1_sb = sb("b1_sb", [1, D])
        sc_in = sb("scalars_sb", [P, 5])
        ex = sb("exp_scales", [P, 4])
        cst = sb("score_constants", [P, 8])
        half = sb("minus_half", [P, 32])
        minus_one = sb("minus_one", [P, T])
        one4 = sb("one_each", [P, T])
        zero4 = sb("zero_each", [P, T])
        phalf = sb("plus_half", [P, 32])

        bank = [pb(f"bank{i}", [P, 512]) for i in range(8)]
        sc = bank[0:4]
        acc_sup, acc_nb, acc_deg, misc = bank[4:8]

        names = """loaded ones_ready setup_chain
            lin_h_ready sig_h_ready ratio_h_ready factor_h_ready h_ready h_t_ready h_rows_ready
            lin_qk_ready sig_qk_ready ratio_qk_ready factor_qk_ready qk_ready hi_ready lo_ready
            stack_t_ready stacks_a stacks_v prologue_chain exps_ready
            adj_landed values_ready0 values_ready1 chunk_used0 chunk_used1 
            sup_t_ready sup_nat_ready sup_saved nb_t_ready deg_s_ready nb_nat_ready nb_saved
            x1_ready deg_reduced deg_added deg_seen b_used0 b_used1 b_static0 b_static1 deg_reduced_b deg_chain
            b_nb_t_ready b_deg_s_ready b_nat_ready b_nat_saved nat_read cat_ready cat_t_psum cat_t_ready z_ready
            relu_ready out_ready out_stored stored_seen nb_a_zero""".split()
        m = {n: sem(n) for n in names}
        scores_ready = [sem(f"scores_ready{t}") for t in range(T)]
        slot_landed = [sem(f"slot_landed{r}") for r in range(RING)]
        chunk_used = [m["chunk_used0"], m["chunk_used1"]]
        values_ready = [m["values_ready0"], m["values_ready1"]]
        att_ready = [sem(f"att_ready{t}") for t in range(T)]
        prod_ready = [sem(f"prod_ready{t}") for t in range(T)]
        b_used = [m["b_used0"], m["b_used1"]]
        b_static = [m["b_static0"], m["b_static1"]]

        with ExitStack() as pro:
            def tmp(name, shape, dt=F32):
                return pro.enter_context(nc.sbuf_tensor(name, shape, dt))

            xt = tmp("x_t_sb", [D + 1, N])
            w_sb = tmp("w_sb", [D + 1, D])
            wqk_sb = tmp("wqk_sb", [D + 1, 2 * D])
            ht = [tmp(f"h_t{i}", [D + 1, CH * P]) for i in range(2)]
            sqh = tmp("sq_h", [P, CH, D])
            sqqk = tmp("sq_qk", [P, 2 * CH, D])
            sigh = tmp("sig_h", [P, CH])
            sigqk = tmp("sig_qk", [P, CH, 2])
            th = tmp("time_h", [P, CH])
            vh = tmp("ratio_h", [P, CH])
            uh = tmp("num_h", [P, CH])
            fh = tmp("factor_h", [P, CH])
            tqk = tmp("time_qk", [P, CH, 2])
            vqk = tmp("ratio_qk", [P, CH, 2])
            uqk = tmp("num_qk", [P, CH, 2])
            fqk = tmp("factor_qk", [P, CH, 2])
            gqk = tmp("scaled_factor_qk", [P, CH, 2])
            e2 = tmp("exp_pair", [P, CH, 2])
            c2 = tmp("scale_pair", [P, CH, 2])
            c2s = tmp("signed_scale_pair", [P, CH, 2])
            qk32 = [tmp(f"qk32_{i}", [P, CH, 2, D]) for i in range(2)]
            natq = [tmp(f"nat_q{i}", [P, CH, 3, D], F16) for i in range(2)]
            natk = [tmp(f"nat_k{i}", [P, CH, 2, D], F16) for i in range(2)]

            lin_h = bank[0][:, :].rearrange("p (t d) -> p t d", d=D)
            hT = [bank[1], bank[2]]
            lin_qk = [bank[3][:, :].rearrange("p (t c d) -> p t c d", c=2, d=D),
                      bank[4][:, :].rearrange("p (t c d) -> p t c d", c=2, d=D)]
            stk, st1, st2 = (bank[i][:, :].bitcast(F16) for i in (5, 6, 7))

            def pow_into(pool, out_, base, exponent):
                return pool.tensor_tensor(out_, base, exponent, ALU.pow)

            with nc.Block() as block:
                @block.sync
                def _(sp):
                    for dst, src in ((sc_in[:, :], scalars), (w_sb[:, :], w_t), (wqk_sb[:, :], wqk_t),
                                     (xt[0:D, :], x_t), (xn[:, :, :], x_nat), (w1_sb[:, :], w1),
                                     (b1_sb[:, :], b1)):
                        sp.dma_start(dst, src).then_inc(m["loaded"], 16)

                @block.gpsimd
                def _(pool):
                    chain = m["setup_chain"]
                    pool.memset(xt[D:D + 1, :], 1.0).then_inc(m["ones_ready"], 1)
                    pool.drain()
                    for b in range(2):
                        pool.memset(ht[b][D:D + 1, :], 1.0).then_inc(m["ones_ready"], 1)
                        pool.drain()
                    pool.memset(half[:, :], -0.5).then_inc(m["ones_ready"], 1)
                    pool.memset(phalf[:, :], 0.5).then_inc(m["ones_ready"], 1)
                    pool.memset(minus_one[:, :], -1.0).then_inc(m["ones_ready"], 1)
                    pool.memset(one4[:, :], 1.0).then_inc(m["ones_ready"], 1)
                    pool.memset(zero4[:, :], 0.0).then_inc(m["ones_ready"], 1)
                    pool.memset(ident[:, :], 0.0).then_inc(chain, 1)
                    pool.wait_ge(chain, 1)
                    pool.affine_select(out=ident[:, :], in_=ident[:, :], compare_op=ALU.not_equal, fill=1.0,
                                       base=0, pattern=[[-1, P]], channel_multiplier=1).then_inc(chain, 1)
                    pool.wait_ge(chain, 2)
                    pool.tensor_copy(ident16[:, :], ident[:, :]).then_inc(m["ones_ready"], 1)
                    pool.memset(ones[:, :], 1.0).then_inc(m["ones_ready"], 1)
                    pool.memset(zero16[:, :], 0.0).then_inc(m["ones_ready"], 1)
                    pool.memset(fold[:, :], 0.0).then_inc(chain, 1)
                    pool.wait_ge(chain, 3)
                    pool.affine_select(out=fold[:, :], in_=fold[:, :], compare_op=ALU.not_equal, fill=1.0,
                                       base=0, pattern=[[-1, D]], channel_multiplier=1).then_inc(chain, 1)
                    pool.wait_ge(chain, 4)
                    pool.affine_select(out=fold[:, :], in_=fold[:, :], compare_op=ALU.not_equal, fill=1.0,
                                       base=-D, pattern=[[-1, D]], channel_multiplier=1)\
                        .then_inc(m["ones_ready"], 1)
                    pool.memset(nb_a[:, 0:T, :], 0.0).then_inc(m["nb_a_zero"], 1)
                    pool.memset(deg_a[:, 0:T], 0.0).then_inc(m["nb_a_zero"], 1)
                    for n in range(NCH + 1):
                        if n < NCH:
                            pool.wait_ge(m["ratio_h_ready"], n + 1)
                            if n >= 1:
                                pool.wait_ge(m["h_ready"], n)
                            pow_into(pool, fh[:, :], vh[:, :], phalf[:, 0:CH]).then_inc(m["factor_h_ready"], 1)
                        if n >= 1:
                            pool.wait_ge(m["ratio_qk_ready"], n)
                            if n >= 2:
                                pool.wait_ge(m["qk_ready"], n - 1)
                            pow_into(pool, fqk[:, :, :], vqk[:, :, :],
                                     phalf[:, 0:2 * CH].rearrange("p (t c) -> p t c", c=2))\
                                .then_inc(m["factor_qk_ready"], 1)

                @block.tensor
                def _(pe):
                    pe.wait_ge(m["loaded"], 16 * 7)
                    pe.wait_ge(m["ones_ready"], 12)
                    for n in range(NCH + 3):
                        if n < NCH:
                            if n >= 1:
                                pe.wait_ge(m["h_ready"], n)
                            for t in range(CH):
                                c = (n * CH + t) * P
                                mm = pe.matmul(lin_h[:, t, :], xt[:, c:c + P], w_sb[:, :], start=True, stop=True)
                            mm.then_inc(m["lin_h_ready"], 1)
                        if 1 <= n <= NCH:
                            k = n - 1
                            pe.wait_ge(m["h_ready"], k + 1)
                            if k >= 1:
                                pe.wait_ge(m["h_rows_ready"], k)
                            for t in range(CH):
                                mm = pe.transpose(hT[t // 4][0:D, (t % 4) * P:(t % 4 + 1) * P],
                                                  h[:, k * CH + t, :], ident[:, :])
                            mm.then_inc(m["h_t_ready"], 1)
                        if n >= 3:
                            k = n - 3
                            pe.wait_ge(m["hi_ready"], k + 1)
                            pe.wait_ge(m["lo_ready"], k + 1)
                            if k >= 1:
                                pe.wait_ge(m["stacks_a"], k)
                                pe.wait_ge(m["stacks_v"], k)
                            for t in range(CH):
                                o = slice(t * P, (t + 1) * P)
                                pe.transpose(stk[:, o], natk[k % 2][:, t, :, :].rearrange("p c d -> p (c d)"),
                                             ident16[:, :])
                                pe.transpose(st1[:, o], natq[k % 2][:, t, 0:2, :].rearrange("p c d -> p (c d)"),
                                             ident16[:, :])
                                mm = pe.transpose(st2[:, o], natq[k % 2][:, t, 1:3, :]
                                                  .rearrange("p c d -> p (c d)"), ident16[:, :])
                            mm.then_inc(m["stack_t_ready"], 1)
                        if 1 <= n <= NCH:
                            k = n - 1
                            pe.wait_ge(m["h_rows_ready"], k + 1)
                            if k >= 1:
                                pe.wait_ge(m["qk_ready"], k)
                            for t in range(CH):
                                mm = pe.matmul(bank[3 + t // 4][:, (t % 4) * P:(t % 4 + 1) * P],
                                               ht[k % 2][:, t * P:(t + 1) * P], wqk_sb[:, :],
                                               start=True, stop=True)
                            mm.then_inc(m["lin_qk_ready"], 1)

                @block.scalar
                def _(act):
                    act.wait_ge(m["loaded"], 16 * 7)
                    act.activation(ex[:, 0:3], sc_in[:, ES:ESK + 1], ACT.Exp).then_inc(m["exps_ready"], 1)

                    for n in range(NCH + 3):
                        if n < NCH:
                            act.wait_ge(m["lin_h_ready"], n + 1)
                            if n >= 1:
                                act.wait_ge(m["ratio_h_ready"], n)
                            act.activation(sigh[:, :], lin_h[:, :, 0], ACT.Sigmoid)
                            act.activation(sqh[:, :, :], lin_h, ACT.Square).then_inc(m["sig_h_ready"], 1)
                        if 1 <= n <= NCH:
                            k = n - 1
                            act.wait_ge(m["h_t_ready"], k + 1)
                            if k >= 2:
                                act.wait_ge(m["lin_qk_ready"], k - 1)
                            for b in range(2):
                                mm = act.activation(ht[k % 2][0:D, b * 512:(b + 1) * 512], hT[b][0:D, :], ACT.Copy)
                            mm.then_inc(m["h_rows_ready"], 1)
                        if 2 <= n < NCH + 2:
                            k = n - 2
                            act.wait_ge(m["qk_ready"], k + 1)
                            if k >= 2:
                                act.wait_ge(m["stack_t_ready"], k - 1)
                            act.activation(natq[k % 2][:, :, 0, :], qk32[k % 2][:, :, 0, :], ACT.Copy)
                            act.activation(natk[k % 2][:, :, 0, :], qk32[k % 2][:, :, 1, :], ACT.Copy)
                            act.activation(natq[k % 2][:, :, 2, :], qk32[k % 2][:, :, 0, :], ACT.Copy)\
                                .then_inc(m["hi_ready"], 1)
                        if 1 <= n <= NCH:
                            k = n - 1
                            act.wait_ge(m["lin_qk_ready"], k + 1)
                            if k >= 1:
                                act.wait_ge(m["ratio_qk_ready"], k)
                            for b in range(2):
                                act.activation(sigqk[:, 4 * b:4 * b + 4, :], lin_qk[b][:, :, :, 0], ACT.Sigmoid)
                                mm = act.activation(sqqk[:, CH * b:CH * b + CH, :], bank[3 + b][:, :]
                                                    .rearrange("p (t d) -> p t d", d=D), ACT.Square)
                            mm.then_inc(m["sig_qk_ready"], 1)
                        if n >= 3:
                            k = n - 3
                            act.wait_ge(m["stack_t_ready"], k + 1)
                            o = slice(k * CH * P, (k + 1) * CH * P)
                            act.activation(kst[:, o], stk, ACT.Copy)
                            act.activation(q1[:, o], st1, ACT.Copy).then_inc(m["stacks_a"], 1)

                @block.vector
                def _(dve):
                    chain = m["prologue_chain"]
                    done = [0]

                    def then(ins):
                        ins.then_inc(chain, 1)
                        done[0] += 1
                        dve.wait_ge(chain, done[0])

                    dve.wait_ge(m["exps_ready"], 1)
                    then(dve.tensor_scalar(cst[:, 0:2], ex[:, 1:3], 1.1, 1.0 / FULL, ALU.add, ALU.mult))
                    then(dve.reciprocal(cst[:, 2:4], cst[:, 0:2]))
                    then(dve.reciprocal(cst[:, 4:5], sc_in[:, ATT_SCALE:ATT_SCALE + 1]))
                    then(dve.tensor_scalar(cst[:, 5:6], cst[:, 4:5], 2.0, None, ALU.mult))
                    then(dve.tensor_tensor(cst[:, 6:7], cst[:, 5:6], sc_in[:, ATT_BIAS:ATT_BIAS + 1], ALU.add))
                    then(dve.tensor_scalar(cst[:, 5:6], cst[:, 5:6], cst[:, 0:1], cst[:, 1:2], ALU.mult, ALU.mult))
                    for c in range(2):
                        then(dve.memset(e2[:, :, c], 1.0))
                        then(dve.memset(c2[:, :, c], 1.0))
                        then(dve.tensor_scalar(c2s[:, :, c], c2[:, :, c], cst[:, 2 + c:3 + c],
                                               (-1.0, 1.0)[c], ALU.mult, ALU.mult))
                        then(dve.tensor_scalar(c2[:, :, c], c2[:, :, c], cst[:, 2 + c:3 + c], None, ALU.mult))
                        then(dve.tensor_scalar(e2[:, :, c], e2[:, :, c], ex[:, 1 + c:2 + c], None, ALU.mult))

                    for n in range(NCH + 3):
                        if n < NCH:
                            dve.wait_ge(m["sig_h_ready"], n + 1)
                            if n >= 1:
                                dve.wait_ge(m["factor_h_ready"], n)
                            dve.tensor_scalar(th[:, :], sigh[:, :], ex[:, 0:1], 1.1, ALU.mult, ALU.add)
                            then(dve.tensor_reduce(uh[:, :], sqh[:, :, 1:D], AX.X, ALU.add))
                            then(dve.tensor_scalar(uh[:, :], uh[:, :], 1e-8, None, ALU.max))
                            dve.reciprocal(uh[:, :], uh[:, :])
                            then(dve.tensor_tensor(vh[:, :], th[:, :], th[:, :], ALU.mult))
                            dve.scalar_tensor_tensor(out=vh[:, :], in0=vh[:, :], scalar=-1.0, in1=uh[:, :],
                                                     op0=ALU.add, op1=ALU.mult).then_inc(m["ratio_h_ready"], 1)
                        if 2 <= n < NCH + 2:
                            k = n - 2
                            dve.wait_ge(m["factor_qk_ready"], k + 1)
                            if k >= 2:
                                dve.wait_ge(m["hi_ready"], k - 1)
                            then(dve.tensor_tensor(gqk[:, :, :], fqk[:, :, :], c2[:, :, :], ALU.mult))
                            for b in range(2):
                                dve.tensor_tensor(qk32[k % 2][:, 4 * b:4 * b + 4, :, 1:D], lin_qk[b][:, :, :, 1:D],
                                                  gqk[:, 4 * b:4 * b + 4, :].unsqueeze(3)
                                                  .to_broadcast([P, 4, 2, D - 1]), ALU.mult)
                            dve.tensor_tensor(qk32[k % 2][:, :, :, 0], tqk[:, :, :], c2s[:, :, :], ALU.mult)\
                                .then_inc(m["qk_ready"], 1)
                        if n >= 3:
                            k = n - 3
                            dve.wait_ge(m["stack_t_ready"], k + 1)
                            dve.tensor_copy(q2[:, k * CH * P:(k + 1) * CH * P], st2).then_inc(m["stacks_v"], 1)
                        if n < NCH:
                            dve.wait_ge(m["factor_h_ready"], n + 1)
                            dve.tensor_tensor(h[:, n * CH:(n + 1) * CH, 1:D], lin_h[:, :, 1:D],
                                              fh[:, :].unsqueeze(2).to_broadcast([P, CH, D - 1]), ALU.mult)
                            dve.tensor_copy(h[:, n * CH:(n + 1) * CH, 0], th[:, :]).then_inc(m["h_ready"], 1)
                        if 2 <= n < NCH + 2:
                            k = n - 2
                            dve.wait_ge(m["hi_ready"], k + 1)
                            dve.tensor_tensor(natq[k % 2][:, :, 1, :], qk32[k % 2][:, :, 0, :],
                                              natq[k % 2][:, :, 0, :], ALU.subtract)
                            dve.tensor_tensor(natk[k % 2][:, :, 1, :], qk32[k % 2][:, :, 1, :],
                                              natk[k % 2][:, :, 0, :], ALU.subtract).then_inc(m["lo_ready"], 1)
                        if 1 <= n <= NCH:
                            k = n - 1
                            dve.wait_ge(m["sig_qk_ready"], k + 1)
                            if k >= 1:
                                dve.wait_ge(m["factor_qk_ready"], k)
                            v3 = "p (t c) -> p t c"
                            then(dve.tensor_tensor(tqk[:, :, :], sigqk[:, :, :], e2[:, :, :], ALU.mult))
                            then(dve.tensor_scalar(tqk[:, :, :], tqk[:, :, :], 1.1, None, ALU.add))
                            then(dve.tensor_reduce(uqk[:, :, :].rearrange("p t c -> p (t c)"),
                                                   sqqk[:, :, 1:D], AX.X, ALU.add))
                            then(dve.tensor_scalar(uqk[:, :, :], uqk[:, :, :], 1e-8, None, ALU.max))
                            dve.reciprocal(uqk[:, :, :], uqk[:, :, :])
                            then(dve.tensor_tensor(vqk[:, :, :], tqk[:, :, :], tqk[:, :, :], ALU.mult))
                            dve.scalar_tensor_tensor(out=vqk[:, :, :], in0=vqk[:, :, :], scalar=-1.0,
                                                     in1=uqk[:, :, :], op0=ALU.add, op1=ALU.mult)\
                                .then_inc(m["ratio_qk_ready"], 1)

        ring = sb("adjacency_ring", [P, RING, T, S])
        prod = [sb(f"product{u}", [P, 2, S]) for u in range(2)]
        hs = sb("h_of_step", [P, T, D])
        xs = sb("x1_of_step", [P, T, D])
        sup_t = sb("support_t", [P, S])
        nb_t = sb("neighbour_t", [P, S])
        deg_p = sb("degree_parts", [P, DSLOTS, S])
        deg_s = sb("degree_sum", [P, S])
        sup_n = sb("support_nat", [P, T, D])
        wa = sb("work_a", [P, T, D])
        wb = sb("work_b", [P, T, D])
        wc = sb("work_c", [P, T, D])
        rc = sb("row_scalars", [P, 8, T])
        nat = sb("sums_nat", [P, T * D + T])
        cat = sb("cat", [P, T, 2 * D])
        cat_t = sb("cat_t", [P, T, P])
        relu = sb("relu", [P, T, D])
        y_out = sb("y_out", [P, T, D])
        cat_psum, z_psum = sc[0], sc[1]

        block = ctx.enter_context(nc.Block())

        def square(idx):
            return adj_sq[bass.ds(idx, 1), :, :].rearrange("s p f -> (s p) f")

        def slot(r):
            return ring[:, r, :, :].rearrange("p t i -> p (t i)")

        def at_reg(i, n):
            return slice(i, i + n) if isinstance(i, int) else bass.ds(i, n)

        def tile_of(sl, t):
            return ring[:, bass.ds(sl, 1), t, :].rearrange("p a i -> p (a i)")

        def value(eng):
            return lambda v: v if isinstance(v, int) else eng.snap(v)

        def upper_count(eng, I):
            return eng.snap(I * (NB - 1) & (NB - 1))

        def squares_before(I):
            return I * (I - 1) >> 1

        def row_of(eng, c, second):
            snap = value(eng)
            if not second:
                return snap(c), snap(c * (NB + 1)), snap(c * (2 * NB - 1) + NB & (2 * NB - 1))
            return snap(c * (NB - 1) + (NB - 1) & (NB - 1)), snap(c * NB + NB), snap(c + 1)


        @block.sync
        def _(sp):
            def relay(k_slot, landed):
                sp.wait_ge(slot_landed[k_slot], landed)
                sp.sem_inc(m["adj_landed"], 1)

            for r in range(RING):
                sp.dma_start(slot(r), adj_sq[r]).then_inc(slot_landed[r], 16)
            for r in range(AHEAD):
                relay(r, 16)
            with sp.Fori(1, STEPS_A // RING) as g:
                for r in range(RING):
                    s = sp.snap(g * RING + r)
                    I = sp.snap((s >> 4) & (NB - 1))
                    at = sp.snap(I * NB + ((s + I) & (NB - 1)), min_val=0, max_val=NB * NB - 1)
                    landed = sp.snap((g + (r + AHEAD) // RING) * 16)
                    used = sp.snap((g - 1) * RING + (r + 3))
                    relay((r + AHEAD) % RING, landed)
                    sp.wait_ge(chunk_used[1], used)
                    sp.dma_start(slot(r), square(at)).then_inc(slot_landed[r], 16)
            sq = sp.alloc_register("square")
            wrap = sp.alloc_register("wrap")
            nxt = sp.alloc_register("next_row")
            late = sp.alloc_register("late")
            sp.reg_mov(sq, 0)

            def issue_b(r, at):
                sp.dma_start(slot(r), square(at)).then_inc(slot_landed[r], 16)
                sp.reg_alu(sq, sq, 1, ALU.add)
                sp.reg_alu(wrap, sq, NB - 1, ALU.bitwise_and)
                sp.reg_alu(wrap, wrap, NB - 1, ALU.add)
                sp.reg_alu(wrap, wrap, 4, ALU.logical_shift_right)
                sp.reg_alu(wrap, wrap, 1, ALU.bitwise_xor)
                sp.reg_alu(nxt, sq, 4, ALU.logical_shift_right)
                sp.reg_alu(late, nxt, NB // 2 - 1, ALU.add)
                sp.reg_alu(late, late, 4, ALU.logical_shift_right)
                sp.reg_alu(late, late, NB, ALU.add)
                sp.reg_alu(nxt, late, nxt, ALU.subtract)
                sp.reg_alu(nxt, nxt, NB + 1, ALU.mult)
                sp.reg_alu(nxt, nxt, sq, ALU.subtract)
                sp.reg_alu(nxt, nxt, wrap, ALU.mult)
                sp.reg_alu(sq, sq, nxt, ALU.add)

            ga = STEPS_A // RING
            for r in range(RING):
                relay((r + AHEAD) % RING, 16 * (ga + (r + AHEAD) // RING))
                sp.wait_ge(chunk_used[1], min((ga - 1) * RING + r + 3, STEPS_A + 1))
                if r == RING - 1:
                    sp.wait_ge(m["deg_reduced"], LOWER)
                issue_b(r, sp.snap(sq, min_val=0, max_val=NB * NB - 1))
            with sp.Fori(0, STEPS_B // RING - 1) as g:
                for r in range(RING):
                    at = sp.snap(sq, min_val=0, max_val=NB * NB - 1)
                    landed = sp.snap((g + (ga + 1) + (r + AHEAD) // RING) * 16)
                    used = sp.snap(g * RING + (r + 2))
                    relay((r + AHEAD) % RING, landed)
                    sp.wait_ge(b_used[1], used)
                    sp.wait_ge(m["deg_reduced_b"], used)
                    issue_b(r, at)
            for r in range(AHEAD, RING):
                relay(r, 16 * (STEPS_A + STEPS_B) // RING)

        @block.tensor
        def _(pe):
            def scores(s1, kcol, qcol, u):
                for t in (2 * u, 2 * u + 1):
                    pe.wait_ge(prod_ready[t], s1)
                    w = kst[:, bass.ds(kcol + t * P, P)]
                    pe.matmul(sc[t][:, :], w, q1[:, bass.ds(qcol, S)], start=True, stop=False)
                    pe.matmul(sc[t][:, :], w, q2[:, bass.ds(qcol, S)], start=False, stop=True)\
                        .then_inc(scores_ready[t], 1)

            def columns(s1):
                I1 = pe.snap((s1 >> 4) & (NB - 1))
                return pe.snap(((s1 + I1) & (NB - 1)) * S), pe.snap(I1 * S)

            def add_to(acc, lhs, rhs):
                return pe.matmul(acc, lhs, rhs, start=False, stop=False, skip_group_check=True)

            def support(u, t, half_):
                return add_to(acc_sup[D * half_:D * half_ + D, :], hs[:, t, :], prod[u][:, t % 2, :])

            def zero(acc):
                pe.matmul(acc[:, :], zero16[:, 0:P], zero16[:, :], start=True, stop=False, skip_group_check=True)

            def upper(s1):
                kcol, qcol = columns(s1)
                for u in range(2):
                    scores(s1, kcol, qcol, u)
                    pe.wait_ge(values_ready[u], s1)
                    support(u, 2 * u, 0)
                    support(u, 2 * u + 1, 1).then_inc(chunk_used[u], 1)

            def lower(s1):
                kcol, qcol = columns(s1)
                sl = pe.snap((s1 - 1) & (RING - 1))
                for u in range(2):
                    scores(s1, kcol, qcol, u)
                    pe.wait_ge(values_ready[u], s1)
                    for t in (2 * u, 2 * u + 1):
                        add_to(acc_nb[0:D, :], xs[:, t, :], tile_of(sl, t))
                        mm = support(u, t, 1)
                    mm.then_inc(chunk_used[u], 1)

            def take(I, has_lower):
                pe.wait_ge(m["sup_t_ready"], I + 1)
                zero(acc_sup)
                if has_lower:
                    pe.wait_ge(m["nb_t_ready"], I)
                    zero(acc_nb)

            def turn(I, has_lower):
                pe.wait_ge(m["sup_saved"], I + 1)
                for c in range(T):
                    mm = pe.matmul(misc[:, c * D:(c + 1) * D], sup_t[:, c * P:(c + 1) * P], fold[:, :],
                                   start=True, stop=True)
                mm.then_inc(m["sup_nat_ready"], 1)
                if has_lower:
                    pe.wait_ge(m["nb_saved"], I)
                    pe.wait_ge(m["deg_s_ready"], I)
                    for c in range(T):
                        o = slice(c * P, (c + 1) * P)
                        pe.matmul(acc_deg[:, c * D:(c + 1) * D], nb_t[0:D, o], fold[0:D, :], start=True, stop=True)
                        mm = pe.matmul(acc_deg[:, T * D + c:T * D + c + 1], deg_s[:, o], ones[:, 0:1],
                                       start=True, stop=True)
                    mm.then_inc(m["nb_nat_ready"], 1)

            for u in range(2):
                pe.sem_inc(chunk_used[u], 1)
                pe.sem_inc(b_used[u], 1)
            pe.sem_inc(m["cat_t_psum"], 1)
            pe.sem_inc(m["b_nat_ready"], 1)
            zero(acc_sup)
            zero(acc_nb)
            for t in range(T):
                w = kst[:, t * P:(t + 1) * P]
                pe.matmul(sc[t][:, :], w, q1[:, 0:S], start=True, stop=False)
                pe.matmul(sc[t][:, :], w, q2[:, 0:S], start=False, stop=True).then_inc(scores_ready[t], 1)
            with pe.Fori(0, NB) as d:
                upper(pe.snap(d + 1))
            take(0, False)

            def row_block(I, is_first, is_last):
                uppers = upper_count(pe, I)
                upper(pe.snap(I * NB + 1))
                turn(0 if is_first else pe.snap(I + (NB - 1) & (NB - 1)), not is_first)
                if not is_last:
                    with pe.Fori(1, uppers) as d:
                        upper(pe.snap(I * NB + d + 1))
                with pe.Fori(0, I) as J:
                    lower(pe.snap(I * NB + uppers + J + 1))
                take(I, True)

            with pe.Fori(1, 2) as I:
                row_block(I, True, False)
            with pe.Fori(2, NB - 1) as I:
                row_block(I, False, False)
            with pe.Fori(NB - 1, NB) as I:
                row_block(I, False, True)
            turn(NB - 1, True)

            def sum_row(c, second):
                K = value(pe)(c * 2 + second)
                _, n0, count = row_of(pe, c, second)
                with pe.Fori(0, count) as d:
                    n = pe.snap(n0 + d)
                    sl = pe.snap(n & (RING - 1))
                    for u in range(2):
                        pe.wait_ge(b_static[u], n + 1)
                        add_to(acc_nb[0:D, :], xs[:, 2 * u, :], tile_of(sl, 2 * u))
                        add_to(acc_nb[D:P, :], xs[:, 2 * u + 1, :], prod[u][:, 0, :]).then_inc(b_used[u], 1)
                pe.wait_ge(m["b_nb_t_ready"], K + 1)
                pe.wait_ge(m["b_deg_s_ready"], K + 1)
                pe.wait_ge(m["b_nat_saved"], K + 1)
                for c in range(T):
                    o = slice(c * P, (c + 1) * P)
                    pe.matmul(misc[:, c * D:(c + 1) * D], nb_t[:, o], fold[:, :], start=True, stop=True)
                    mm = pe.matmul(misc[:, T * D + c:T * D + c + 1], deg_s[:, o], ones[:, 0:1],
                                   start=True, stop=True)
                mm.then_inc(m["b_nat_ready"], 1)
                zero(acc_nb)

            def linear_row(done):
                pe.wait_ge(m["cat_ready"], done)
                for c in range(T):
                    mm = pe.transpose(cat_psum[:, c * P:(c + 1) * P], cat[:, c, :], ident[:, :])
                mm.then_inc(m["cat_t_psum"], 1)
                pe.wait_ge(m["cat_t_ready"], done)
                for c in range(T):
                    pe.matmul(z_psum[:, c * D:(c + 1) * D], cat_t[:, c, :], w1_sb[:, :], start=True, stop=False)
                    mm = pe.matmul(z_psum[:, c * D:(c + 1) * D], ones[0:1, :], b1_sb[:, :], start=False, stop=True)
                mm.then_inc(m["z_ready"], 1)

            sum_row(0, 0)
            sum_row(0, 1)
            linear_row(1)
            with pe.Fori(1, NB // 2) as c:
                sum_row(c, 0)
                linear_row(pe.snap(c * 2))
                sum_row(c, 1)
                linear_row(pe.snap(c * 2 + 1))
            linear_row(NB)

        @block.scalar
        def _(act):
            def sigmoids(s1, u):
                for t in (2 * u, 2 * u + 1):
                    act.wait_ge(scores_ready[t], s1 + 1)
                    act.activation(sc[t][:, :], sc[t][:, :], ACT.Sigmoid, bias=cst[:, 6:7],
                                   scale=cst[:, 5:6]).then_inc(att_ready[t], 1)

            def step(s, J, with_x1):
                j = value(act)(J * T)
                for u in range(2):
                    half_of = slice(2 * u, 2 * u + 2)
                    act.wait_ge(chunk_used[u], s + 1)
                    if with_x1:
                        if u == 0:
                            act.wait_ge(m["x1_ready"], J + 2)
                        act.activation(xs[:, half_of, :], xn[:, bass.ds(j + 2 * u, 2), :], ACT.Copy)
                    act.activation(hs[:, half_of, :], h[:, bass.ds(j + 2 * u, 2), :], ACT.Copy)\
                        .then_inc(values_ready[u], 1)
                    sigmoids(s + 1, u)

            def take(I, has_lower):
                act.wait_ge(chunk_used[1], I * NB + (NB + 1))
                act.activation(sup_t[:, :], acc_sup[:, :], ACT.Copy).then_inc(m["sup_t_ready"], 1)
                if has_lower:
                    act.activation(nb_t[0:D, :], acc_nb[0:D, :], ACT.Copy).then_inc(m["nb_t_ready"], 1)

            def save(I, has_lower):
                act.wait_ge(m["sup_nat_ready"], I + 1)
                act.wait_ge(m["x1_ready"], I + 1)
                act.activation(sup_n[:, :, :], misc[:, 0:T * D].rearrange("p (t d) -> p t d", d=D), ACT.Copy)\
                    .then_inc(m["sup_saved"], 1)
                if has_lower:
                    act.wait_ge(m["nb_nat_ready"], I)
                    act.activation(nb_a[:, bass.ds(I * T, T), :],
                                   acc_deg[:, 0:T * D].rearrange("p (t d) -> p t d", d=D), ACT.Copy)
                    act.activation(deg_a[:, bass.ds(I * T, T)], acc_deg[:, T * D:T * D + T], ACT.Copy)\
                        .then_inc(m["nb_saved"], 1)

            act.sem_inc(m["sup_saved"], 1)
            act.sem_inc(m["b_nat_saved"], 1)
            act.sem_inc(m["nb_saved"], 1)
            sigmoids(0, 0)
            sigmoids(0, 1)
            with act.Fori(0, NB) as J:
                step(J, J, False)
            take(0, False)

            def row_block(I, is_first, is_last):
                uppers = upper_count(act, I)
                step(act.snap(I * NB), I, False)
                save(0 if is_first else act.snap(I + (NB - 1) & (NB - 1)), not is_first)
                if not is_last:
                    with act.Fori(1, uppers) as d:
                        step(act.snap(I * NB + d), act.snap((I + d) & (NB - 1)), False)
                with act.Fori(0, I) as J:
                    step(act.snap(I * NB + uppers + J), J, True)
                take(I, True)

            with act.Fori(1, 2) as I:
                row_block(I, True, False)
            with act.Fori(2, NB - 1) as I:
                row_block(I, False, False)
            with act.Fori(NB - 1, NB) as I:
                row_block(I, False, True)
            save(NB - 1, True)

            def sum_row(c, second):
                K = value(act)(c * 2 + second)
                I, n0, count = row_of(act, c, second)
                with act.Fori(0, count) as d:
                    n = act.snap(n0 + d)
                    sl = act.snap(n & (RING - 1))
                    J = act.snap((I + d) & (NB - 1))
                    jt = act.snap(J * T)
                    act.wait_ge(m["adj_landed"], n + (STEPS_A + 1))
                    act.wait_ge(m["x1_ready"], J + 2)
                    for u in range(2):
                        act.wait_ge(b_used[u], n + 1)
                        act.activation(xs[:, 2 * u:2 * u + 2, :], xn[:, bass.ds(jt + 2 * u, 2), :], ACT.Copy)
                        act.activation(prod[u][:, 0, :], tile_of(sl, 2 * u + 1), ACT.Copy)\
                            .then_inc(b_static[u], 1)
                act.wait_ge(b_used[1], n0 + count + 1)
                act.activation(nb_t[:, :], acc_nb[:, :], ACT.Copy).then_inc(m["b_nb_t_ready"], 1)
                act.wait_ge(m["b_nat_ready"], K + 2)
                act.wait_ge(m["nat_read"], K + 1)
                act.activation(nat[:, :], misc[:, 0:T * D + T], ACT.Copy).then_inc(m["b_nat_saved"], 1)

            def linear_row(done):
                act.wait_ge(m["cat_t_psum"], done + 1)
                act.activation(cat_t[:, :, :], cat_psum[:, :].rearrange("p (t i) -> p t i", t=T), ACT.Copy)\
                    .then_inc(m["cat_t_ready"], 1)
                act.wait_ge(m["z_ready"], done)
                act.wait_ge(m["out_ready"], done)
                act.activation(relu[:, :, :], z_psum[:, 0:T * D].rearrange("p (t d) -> p t d", d=D), ACT.Relu)\
                    .then_inc(m["relu_ready"], 1)

            sum_row(0, 0)
            sum_row(0, 1)
            linear_row(1)
            with act.Fori(1, NB // 2) as c:
                sum_row(c, 0)
                linear_row(act.snap(c * 2))
                sum_row(c, 1)
                linear_row(act.snap(c * 2 + 1))
            linear_row(NB)

        @block.vector
        def _(dve):
            def product(s, sl, u):
                dve.wait_ge(chunk_used[u], s + 1)
                for t in (2 * u, 2 * u + 1):
                    dve.wait_ge(att_ready[t], s + 1)
                    dve.tensor_tensor(prod[u][:, t % 2, :], sc[t][:, :], tile_of(sl, t), ALU.mult)\
                        .then_inc(prod_ready[t], 1)

            def degrees(sl, part, lo=0, hi=S):
                return dve.tensor_reduce(deg_p[:, bass.ds(part, 1), lo:hi].rearrange("p a i -> p (a i)"),
                                         ring[:, bass.ds(sl, 1), :, lo:hi].rearrange("p a t i -> p i (a t)"),
                                         AX.X, ALU.add)

            def upper(s):
                sl = dve.snap(s & (RING - 1))
                dve.wait_ge(m["adj_landed"], s + 1)
                for u in range(2):
                    product(s, sl, u)

            with dve.Fori(0, NB) as J:
                upper(J)
            with dve.Fori(1, NB) as I:
                uppers = upper_count(dve, I)
                with dve.Fori(0, uppers) as d:
                    upper(dve.snap(I * NB + d))
                with dve.Fori(0, I) as J:
                    s = dve.snap(I * NB + uppers + J)
                    n = dve.snap(squares_before(I) + J)
                    sl = dve.snap(s & (RING - 1))
                    part = dve.snap(n & (DSLOTS - 1))
                    dve.wait_ge(m["adj_landed"], s + 1)
                    product(s, sl, 0)
                    dve.wait_ge(m["deg_added"], n + 1)
                    degrees(sl, part, 0, S // 2)
                    product(s, sl, 1)
                    degrees(sl, part, S // 2, S).then_inc(m["deg_reduced"], 1)

            chain = m["deg_chain"]

            def deg_add(n, K):
                dve.wait_ge(m["deg_reduced_b"], n + 1)
                dve.wait_ge(chain, n + K)
                dve.tensor_tensor(acc_deg[:, :], acc_deg[:, :],
                                  deg_p[:, bass.ds((n + (DSLOTS - 1)) & (DSLOTS - 1), 1), :]
                                  .rearrange("p a i -> p (a i)"), ALU.add)\
                    .then_inc(chain, 1)

            dve.sem_inc(m["deg_reduced_b"], 1)
            dve.wait_ge(m["nb_saved"], NB)
            dve.wait_ge(m["deg_added"], DSLOTS + LOWER)
            def degree_row(c, second):
                K = value(dve)(c * 2 + second)
                _, n0, count = row_of(dve, c, second)
                dve.wait_ge(m["adj_landed"], n0 + (STEPS_A + 1))
                degrees(n0 & (RING - 1), n0 & (DSLOTS - 1)).then_inc(m["deg_reduced_b"], 1)
                dve.drain()
                dve.memset(acc_deg[:, :], 0.0).then_inc(chain, 1)
                with dve.Fori(1, count + 1) as d:
                    n = dve.snap(n0 + d)
                    with dve.If(d < count):
                        dve.wait_ge(m["adj_landed"], n + (STEPS_A + 1))
                        degrees(n & (RING - 1), n & (DSLOTS - 1)).then_inc(m["deg_reduced_b"], 1)
                    deg_add(n, K)
                dve.wait_ge(chain, n0 + count + K + 1)
                dve.wait_ge(m["b_nat_ready"], K + 1)
                dve.tensor_copy(deg_s[:, :], acc_deg[:, :]).then_inc(m["b_deg_s_ready"], 1)

            with dve.Fori(0, NB // 2) as c:
                degree_row(c, 0)
                degree_row(c, 1)

        @block.gpsimd
        def _(pool):
            def then(ins):
                pool.drain()

            def row(i):
                return rc[:, i, :]

            def spread(i):
                return rc[:, i, :].unsqueeze(2).to_broadcast([P, T, D])

            def row_sum(buf, out_row):
                w = D // 2
                while w >= 1:
                    dst = buf[:, :, 0:w] if w > 1 else row(out_row).unsqueeze(2)
                    then(pool.tensor_tensor(dst, buf[:, :, 0:w], buf[:, :, w:2 * w], ALU.add))
                    w //= 2

            def layernorm(src, last_out):
                w = D // 2
                then(pool.tensor_tensor(wb[:, :, 0:w], src[:, :, 0:w], src[:, :, w:D], ALU.add))
                while w > 1:
                    w //= 2
                    dst = wb[:, :, 0:w] if w > 1 else row(0).unsqueeze(2)
                    then(pool.tensor_tensor(dst, wb[:, :, 0:w], wb[:, :, w:2 * w], ALU.add))
                then(pool.tensor_scalar(row(1), row(0), 1.0 / D, None, ALU.mult))
                then(pool.tensor_tensor(wc[:, :, :], src, spread(1), ALU.subtract))
                then(pool.tensor_tensor(wb[:, :, :], wc[:, :, :], wc[:, :, :], ALU.mult))
                row_sum(wb, 2)
                then(pool.tensor_scalar(row(3), row(2), 1.0 / D, EPS, ALU.mult, ALU.add))
                then(pool.tensor_tensor(row(4), row(3), half[:, 0:T], ALU.pow))
                return pool.tensor_tensor(last_out, wc[:, :, :], spread(4), ALU.mult)

            def finish_x1(I):
                x_blk = xn[:, at_reg(I * T, T), :]
                pool.wait_ge(m["sup_saved"], I + 2)
                then(pool.tensor_tensor(wa[:, :, :], sup_n[:, :, :], sup_n[:, :, :], ALU.mult))
                then(pool.tensor_scalar(row(5), wa[:, :, 0], -2.0, None, ALU.mult))
                row_sum(wa, 6)
                then(pool.tensor_tensor(row(5), row(5), row(6), ALU.add))
                pool.tensor_scalar(row(6), row(5), 0.0, None, ALU.max)
                then(pool.tensor_scalar(row(7), row(5), 0.0, None, ALU.min))
                then(pool.tensor_tensor(row(6), row(6), row(7), ALU.subtract))
                then(pool.tensor_scalar(row(6), row(6), 1e-8, None, ALU.max))
                then(pool.tensor_tensor(row(5), row(6), half[:, 0:T], ALU.pow))
                then(pool.tensor_tensor(wa[:, :, :], sup_n[:, :, :], spread(5), ALU.mult))
                then(pool.tensor_tensor(wa[:, :, :], wa[:, :, :], x_blk, ALU.add))
                layernorm(wa[:, :, :], x_blk).then_inc(m["x1_ready"], 1)
                pool.drain()

            pool.sem_inc(m["x1_ready"], 1)
            pool.sem_inc(m["nat_read"], 1)
            pool.sem_inc(m["out_ready"], 1)
            pool.sem_inc(m["deg_added"], DSLOTS)
            finish_x1(0)
            with pool.Fori(1, NB) as I:
                pool.wait_ge(m["nb_saved"], I)
                pool.sem_inc(m["deg_seen"], 1)
                pool.memset(deg_s[:, :], 0.0)
                pool.drain()
                with pool.Fori(0, I) as J:
                    n = pool.snap(squares_before(I) + J)
                    pool.wait_ge(m["deg_reduced"], n + 1)
                    pool.sem_inc(m["deg_seen"], 1)
                    pool.tensor_tensor(deg_s[:, :], deg_s[:, :],
                                       deg_p[:, bass.ds(n & (DSLOTS - 1), 1), :].rearrange("p a i -> p (a i)"),
                                       ALU.add).then_inc(m["deg_added"], 1)
                    pool.drain()
                pool.sem_inc(m["deg_s_ready"], 1)
                finish_x1(I)

            def neighbours(done, I):
                x_blk = xn[:, at_reg(I * T, T), :]
                pool.wait_ge(m["cat_t_psum"], done)
                pool.wait_ge(m["b_nat_saved"], done + 1)
                pool.tensor_tensor(row(0), nat[:, T * D:T * D + T], one4[:, :], ALU.add)
                pool.tensor_tensor(cat[:, :, 0:D], x_blk, zero4[:, :].unsqueeze(2).to_broadcast([P, T, D]), ALU.add)
                then(pool.tensor_tensor(wa[:, :, :], nat[:, 0:T * D].rearrange("p (t d) -> p t d", d=D),
                                        nb_a[:, at_reg(I * T, T), :], ALU.add))
                pool.sem_inc(m["nat_read"], 1)
                then(pool.tensor_tensor(row(0), row(0), deg_a[:, at_reg(I * T, T)], ALU.add))
                pool.tensor_tensor(wa[:, :, :], wa[:, :, :], x_blk, ALU.add)
                then(pool.tensor_scalar(row(0), row(0), 1.0, None, ALU.max))
                then(pool.tensor_tensor(row(1), row(0), minus_one[:, :], ALU.pow))
                pool.tensor_tensor(cat[:, :, D:2 * D], wa[:, :, :], spread(1), ALU.mult)\
                    .then_inc(m["cat_ready"], 1)
                pool.drain()

            def finish_x2(done, I):
                pool.wait_ge(m["relu_ready"], done)
                then(pool.tensor_tensor(wa[:, :, :], relu[:, :, :], relu[:, :, :], ALU.mult))
                row_sum(wa, 5)
                then(pool.tensor_tensor(row(6), row(5), phalf[:, 0:T], ALU.pow))
                then(pool.tensor_scalar(row(6), row(6), 1e-12, None, ALU.max))
                then(pool.tensor_tensor(row(7), row(6), minus_one[:, :], ALU.pow))
                then(pool.tensor_tensor(wa[:, :, :], relu[:, :, :], spread(7), ALU.mult))
                then(pool.tensor_tensor(wa[:, :, :], wa[:, :, :], xn[:, at_reg(I * T, T), :], ALU.add))
                layernorm(wa[:, :, :], y_out[:, :, :]).then_inc(m["out_ready"], 1)
                pool.drain()
                pool.dma_start(out[at_reg(I, 1), :, :].rearrange("s p f -> (s p) f"),
                               y_out[:, :, :].rearrange("p t d -> p (t d)")).then_inc(m["out_stored"], 16)
                pool.wait_ge(m["out_stored"], done * 16)
                pool.sem_inc(m["stored_seen"], 1)

            neighbours(1, 0)
            neighbours(2, NB - 1)
            finish_x2(1, 0)
            with pool.Fori(1, NB // 2) as c:
                rows = pool.snap(c * 2)
                small = pool.snap(c * (NB - 1) + (NB - 1) & (NB - 1))
                neighbours(rows + 1, c)
                finish_x2(rows, (small + 1) & (NB - 1))
                neighbours(rows + 2, small)
                finish_x2(rows + 1, c)
            finish_x2(NB, NB // 2)


def kernel(x, adj, L0_gnn_W, L0_gnn_b, L0_gnn_scale, L0_gnn_Wq, L0_gnn_bq, L0_gnn_scale_q, L0_gnn_Wk, L0_gnn_bk,
           L0_gnn_scale_k, L0_gnn_att_bias, L0_gnn_att_scale, L1_gnn_W, L1_gnn_b):
    import numpy as np
    import concourse.bacc as bacc
    from concourse.bass_utils import run_bass_kernel_spmd

    nc = bacc.Bacc("TRN2", target_bir_lowering=False, num_devices=1)
    x = np.asarray(x)
    scalars = np.stack([np.asarray(v).reshape(()) for v in
                        (L0_gnn_scale, L0_gnn_scale_q, L0_gnn_scale_k, L0_gnn_att_bias, L0_gnn_att_scale)])
    arrays = {
        "adj_sq": np.ascontiguousarray(np.asarray(adj).reshape(NB, S, NB, T, P).transpose(0, 2, 4, 3, 1))
        .reshape(NB * NB, P, T * S),
        "x_nat": np.ascontiguousarray(x.reshape(NT, P, D).transpose(1, 0, 2)),
        "x_t": np.ascontiguousarray(x.T),
        "w_t": np.concatenate([np.asarray(L0_gnn_W).T, np.asarray(L0_gnn_b)[None]]),
        "wqk_t": np.concatenate([np.concatenate([np.asarray(L0_gnn_Wq).T, np.asarray(L0_gnn_Wk).T], 1),
                                 np.concatenate([np.asarray(L0_gnn_bq), np.asarray(L0_gnn_bk)])[None]]),
        "w1": np.ascontiguousarray(np.asarray(L1_gnn_W)),
        "b1": np.ascontiguousarray(np.asarray(L1_gnn_b).reshape(1, D)),
        "scalars": np.ascontiguousarray(np.broadcast_to(scalars[None], (P, 5))),
    }
    args = [nc.dram_tensor(n, a.shape, F32, kind="ExternalInput").ap() for n, a in arrays.items()]
    out = nc.dram_tensor("x2", (NB, P, T * D), F32, kind="ExternalOutput").ap()
    two_layers(nc, *args, out)
    got = run_bass_kernel_spmd(nc, [arrays], core_ids=[0]).results[0]["x2"]
    return np.ascontiguousarray(np.asarray(got).reshape(NB, P, T, D).transpose(0, 2, 1, 3)).reshape(N, D)
```

```python
from contextlib import ExitStack

import concourse.bass as bass
from concourse import mybir

F32 = mybir.dt.float32
F16 = mybir.dt.float16
ALU = mybir.AluOpType
ACT = mybir.ActivationFunctionType
AX = mybir.AxisListType

P = 128
N = 8192
D = 64
NT = N // P
S = 512
NB = N // S
T = S // P
STEPS_A = NB * NB
STEPS_B = NB * (NB + 1) // 2
DSLOTS = 4
LOWER = NB * (NB - 1) // 2
RING = 8
AHEAD = 5
HEAD = RING - 1 - N // (T * S)
CH = 8
NCH = NT // CH
FULL = 32768.0
EPS = 1e-5
(ES, ESQ, ESK, ATT_BIAS, ATT_SCALE) = range(5)


def two_layers(nc, adj_sq, x_nat, x_t, w_t, wqk_t, w1, b1, scalars, out):
    ctx = ExitStack()
    with ctx:
        def sb(name, shape, dt=F32):
            return ctx.enter_context(nc.sbuf_tensor(name, shape, dt))

        def sem(name):
            return ctx.enter_context(nc.semaphore(name))

        def pb(name, shape, dt=F32):
            return ctx.enter_context(nc.psum_tensor(name, shape, dt))

        ring = sb("adjacency_ring", [P, RING, T, S])
        kst = sb("k_stack", [P, N], F16)
        q1 = sb("q_stack", [P, N], F16)
        q2 = sb("q_stack_swapped", [P, N], F16)
        h = sb("h", [P, NT, D])
        xn = sb("x_then_x1", [P, NT, D])
        nb_a = sb("neighbour_sum_a", [P, NT, D])
        deg_a = sb("degree_a", [P, NT])
        ident = sb("ident", [P, P])
        ident16 = sb("ident16", [P, P], F16)
        fold = sb("fold", [P, D])
        ones = sb("ones", [P, P])
        zero16 = sb("zero16", [P, S], F16)
        w1_sb = sb("w1_sb", [P, D])
        b1_sb = sb("b1_sb", [1, T * D])
        sc_in = sb("scalars_sb", [P, 5])
        ex = sb("exp_scales", [P, 4])
        cst = sb("score_constants", [P, 8])
        half = sb("minus_half", [P, 32])
        minus_one = sb("minus_one", [P, T])
        one4 = sb("one_each", [P, T])
        zero4 = sb("zero_each", [P, T])
        phalf = sb("plus_half", [P, 32])

        bank = [pb(f"bank{i}", [P, 512]) for i in range(8)]
        sc = bank[0:4]
        acc_sup, acc_nb, acc_deg, misc = bank[4:8]

        names = """loaded x_loaded rest_loaded ones_ready setup_chain
            lin_h_ready sig_h_ready ratio_h_ready factor_h_ready h_ready h_t_ready h_rows_ready
            lin_qk_ready sig_qk_ready ratio_qk_ready factor_qk_ready qk_ready hi_ready lo_ready
            stack_t_ready stacks_a prologue_chain exps_ready
            adj_landed values_ready0 values_ready1 chunk_used0 chunk_used1
            sup_t_ready sup_nat_ready sup_saved nb_t_ready deg_s_ready nb_nat_ready nb_saved
            x1_ready deg_reduced deg_added deg_seen b_used0 b_used1 b_static0 b_static1 deg_added_b
            last_chain last_base last_root last_ready last_stored
            b_nb_t_ready b_deg_s_ready b_nat_ready b_nat_saved nat_read cat_ready cat_t_psum cat_t_ready z_ready
            relu_part relu_ready relu_seen out_ready out_stored stored_seen nb_a_zero""".split()
        m = {n: sem(n) for n in names}
        scores_ready = [sem(f"scores_ready{t}") for t in range(T)]
        slot_landed = [sem(f"slot_landed{r}") for r in range(RING)]
        chunk_used = [m["chunk_used0"], m["chunk_used1"]]
        values_ready = [m["values_ready0"], m["values_ready1"]]
        att_ready = [sem(f"att_ready{t}") for t in range(T)]
        prod_ready = [sem(f"prod_ready{t}") for t in range(T)]
        b_used = [m["b_used0"], m["b_used1"]]
        b_static = [m["b_static0"], m["b_static1"]]

        with ExitStack() as pro:
            def tmp(name, shape, dt=F32):
                return pro.enter_context(nc.sbuf_tensor(name, shape, dt))

            xt = ring[0:D + 1, HEAD:RING - 1, :, :].rearrange("p r t i -> p (r t i)")
            qk32_at = ring[:, RING - 1, :, :].rearrange("p t i -> p (t i)")
            w_sb = tmp("w_sb", [D + 1, D])
            wqk_sb = tmp("wqk_sb", [D + 1, 2 * D])
            ht = [tmp(f"h_t{i}", [D + 1, CH * P]) for i in range(2)]
            sqh = tmp("sq_h", [P, CH, D])
            sqqk = tmp("sq_qk", [P, 2 * CH, D])
            sigh = tmp("sig_h", [P, CH])
            sigqk = tmp("sig_qk", [P, CH, 2])
            th = tmp("time_h", [P, CH])
            vh = tmp("ratio_h", [P, CH])
            uh = tmp("num_h", [P, CH])
            fh = tmp("factor_h", [P, CH])
            tqk = tmp("time_qk", [P, CH, 2])
            vqk = tmp("ratio_qk", [P, CH, 2])
            uqk = tmp("num_qk", [P, CH, 2])
            fqk = tmp("factor_qk", [P, CH, 2])
            gqk = tmp("scaled_factor_qk", [P, CH, 2])
            e2 = tmp("exp_pair", [P, CH, 2])
            c2 = tmp("scale_pair", [P, CH, 2])
            c2s = tmp("signed_scale_pair", [P, CH, 2])
            qk32 = [qk32_at[:, i * CH * 2 * D:(i + 1) * CH * 2 * D].rearrange("p (t c d) -> p t c d", c=2, d=D)
                    for i in range(2)]
            parts16 = [tmp(f"float16_parts{i}", [P, CH, 2, 2, D], F16) for i in range(2)]

            lin_h = bank[0][:, :].rearrange("p (t d) -> p t d", d=D)
            hT = bank[1]
            lin_sb = [tmp(f"lin_qk_sb{i}", [P, CH, 2, D]) for i in range(2)]
            lin_qk = [bank[3][:, :].rearrange("p (t c d) -> p t c d", c=2, d=D),
                      bank[4][:, :].rearrange("p (t c d) -> p t c d", c=2, d=D)]
            st_q, st_k = (bank[i][:, :].bitcast(F16) for i in (5, 6))

            def pow_into(pool, out_, base, exponent):
                return pool.tensor_tensor(out_, base, exponent, ALU.pow)

            with nc.Block() as block:
                @block.sync
                def _(sp):
                    for dst, src in ((sc_in[:, :], scalars), (w_sb[:, :], w_t), (xt[:, 0:CH * P], x_t[:, 0:CH * P]),
                                     (wqk_sb[:, :], wqk_t)):
                        sp.dma_start(dst, src).then_inc(m["loaded"], 16)
                    sp.dma_start(xt[:, CH * P:N], x_t[:, CH * P:N]).then_inc(m["x_loaded"], 16)
                    for dst, src in ((w1_sb[:, :], w1), (b1_sb[:, :], b1), (xn[:, :, :], x_nat)):
                        sp.dma_start(dst, src).then_inc(m["rest_loaded"], 16)
                    for r in range(HEAD):
                        sp.dma_start(ring[:, r, :, :].rearrange("p t i -> p (t i)"), adj_sq[r]).then_inc(slot_landed[r], 16)
                    sp.wait_ge(m["rest_loaded"], 16 * 3)

                @block.gpsimd
                def _(pool):
                    chain = m["setup_chain"]
                    for b in range(2):
                        pool.memset(ht[b][D:D + 1, :], 1.0).then_inc(m["ones_ready"], 1)
                        pool.drain()
                    pool.memset(half[:, :], -0.5).then_inc(m["ones_ready"], 1)
                    pool.memset(phalf[:, :], 0.5).then_inc(m["ones_ready"], 1)
                    pool.memset(minus_one[:, :], -1.0).then_inc(m["ones_ready"], 1)
                    pool.memset(one4[:, :], 1.0).then_inc(m["ones_ready"], 1)
                    pool.memset(zero4[:, :], 0.0).then_inc(m["ones_ready"], 1)
                    pool.memset(ident[:, :], 0.0).then_inc(chain, 1)
                    pool.wait_ge(chain, 1)
                    pool.affine_select(out=ident[:, :], in_=ident[:, :], compare_op=ALU.not_equal, fill=1.0,
                                       base=0, pattern=[[-1, P]], channel_multiplier=1).then_inc(chain, 1)
                    pool.wait_ge(chain, 2)
                    pool.tensor_copy(ident16[:, :], ident[:, :]).then_inc(m["ones_ready"], 1)
                    pool.memset(ones[:, :], 1.0).then_inc(m["ones_ready"], 1)
                    pool.memset(zero16[:, :], 0.0).then_inc(m["ones_ready"], 1)
                    pool.memset(fold[:, :], 0.0).then_inc(chain, 1)
                    pool.wait_ge(chain, 3)
                    pool.affine_select(out=fold[:, :], in_=fold[:, :], compare_op=ALU.not_equal, fill=1.0,
                                       base=0, pattern=[[-1, D]], channel_multiplier=1).then_inc(chain, 1)
                    pool.wait_ge(chain, 4)
                    pool.affine_select(out=fold[:, :], in_=fold[:, :], compare_op=ALU.not_equal, fill=1.0,
                                       base=-D, pattern=[[-1, D]], channel_multiplier=1)\
                        .then_inc(m["ones_ready"], 1)
                    pool.memset(nb_a[:, 0:T, :], 0.0).then_inc(m["nb_a_zero"], 1)
                    pool.memset(deg_a[:, 0:T], 0.0).then_inc(m["nb_a_zero"], 1)
                    for n in range(NCH + 1):
                        if n < NCH:
                            pool.wait_ge(m["ratio_h_ready"], n + 1)
                            if n >= 1:
                                pool.wait_ge(m["h_ready"], n)
                            pow_into(pool, fh[:, :], vh[:, :], phalf[:, 0:CH]).then_inc(m["factor_h_ready"], 1)
                        if n >= 1:
                            pool.wait_ge(m["ratio_qk_ready"], n)
                            if n >= 2:
                                pool.wait_ge(m["qk_ready"], n - 1)
                            pow_into(pool, fqk[:, :, :], vqk[:, :, :],
                                     phalf[:, 0:2 * CH].rearrange("p (t c) -> p t c", c=2))\
                                .then_inc(m["factor_qk_ready"], 1)

                @block.tensor
                def _(pe):
                    pe.wait_ge(m["loaded"], 16 * 4)
                    pe.wait_ge(m["ones_ready"], 11)
                    for n in range(NCH + 3):
                        if n < NCH:
                            if n == 1:
                                pe.wait_ge(m["x_loaded"], 16)
                            if n >= 1:
                                pe.wait_ge(m["h_ready"], n)
                            for t in range(CH):
                                c = (n * CH + t) * P
                                mm = pe.matmul(lin_h[:, t, :], xt[:, c:c + P], w_sb[:, :], start=True, stop=True)
                            mm.then_inc(m["lin_h_ready"], 1)
                        if 1 <= n <= NCH:
                            k = n - 1
                            pe.wait_ge(m["h_rows_ready"], k + 1)
                            if k >= 1:
                                pe.wait_ge(m["sig_qk_ready"], k)
                            for t in range(CH):
                                mm = pe.matmul(bank[3 + t // 4][:, (t % 4) * P:(t % 4 + 1) * P],
                                               ht[k % 2][:, t * P:(t + 1) * P], wqk_sb[:, :],
                                               start=True, stop=True)
                            mm.then_inc(m["lin_qk_ready"], 1)
                        if n >= 3:
                            k = n - 3
                            pe.wait_ge(m["hi_ready"], k + 1)
                            pe.wait_ge(m["lo_ready"], k + 1)
                            if k >= 1:
                                pe.wait_ge(m["stacks_a"], k)
                            for t in range(CH):
                                o = slice(t * P, (t + 1) * P)
                                for c, st in enumerate((st_q, st_k)):
                                    mm = pe.transpose(st[:, o], parts16[k % 2][:, t, c, :, :]
                                                      .rearrange("p c d -> p (c d)"), ident16[:, :])
                            mm.then_inc(m["stack_t_ready"], 1)
                        if n < NCH:
                            k = n
                            pe.wait_ge(m["h_ready"], k + 1)
                            if k >= 1:
                                pe.wait_ge(m["h_rows_ready"], k)
                            for i in range(CH // 2):
                                t = k * CH + 2 * i
                                mm = pe.transpose(hT[:, i * P:(i + 1) * P],
                                                  h[:, t:t + 2, :].rearrange("p t d -> p (t d)"), ident[:, :])
                            mm.then_inc(m["h_t_ready"], 1)

                @block.scalar
                def _(act):
                    act.wait_ge(m["loaded"], 16 * 4)
                    act.activation(ex[:, 0:3], sc_in[:, ES:ESK + 1], ACT.Exp).then_inc(m["exps_ready"], 1)

                    for n in range(NCH + 4):
                        if n < NCH:
                            act.wait_ge(m["lin_h_ready"], n + 1)
                            if n >= 1:
                                act.wait_ge(m["ratio_h_ready"], n)
                            act.activation(sigh[:, :], lin_h[:, :, 0], ACT.Sigmoid)
                            act.activation(sqh[:, :, :], lin_h, ACT.Square).then_inc(m["sig_h_ready"], 1)
                        if n >= 4:
                            k = n - 4
                            act.wait_ge(m["stack_t_ready"], k + 1)
                            o = slice(k * CH * P, (k + 1) * CH * P)
                            act.activation(kst[:, o], st_k, ACT.Copy)
                            act.activation(q1[:, o], st_q, ACT.Copy).then_inc(m["stacks_a"], 1)
                        if 1 <= n <= NCH:
                            k = n - 1
                            act.wait_ge(m["lin_qk_ready"], k + 1)
                            if k >= 1:
                                act.wait_ge(m["ratio_qk_ready"], k)
                            if k >= 2:
                                act.wait_ge(m["qk_ready"], k - 1)
                            for b in range(2):
                                act.activation(sigqk[:, 4 * b:4 * b + 4, :], lin_qk[b][:, :, :, 0], ACT.Sigmoid)
                                act.activation(sqqk[:, CH * b:CH * b + CH, :], bank[3 + b][:, :]
                                               .rearrange("p (t d) -> p t d", d=D), ACT.Square)
                                mm = act.activation(lin_sb[k % 2][:, 4 * b:4 * b + 4, :, :], lin_qk[b], ACT.Copy)
                            mm.then_inc(m["sig_qk_ready"], 1)
                        if 2 <= n < NCH + 2:
                            k = n - 2
                            act.wait_ge(m["qk_ready"], k + 1)
                            if k >= 2:
                                act.wait_ge(m["stack_t_ready"], k - 1)
                            act.activation(parts16[k % 2][:, :, :, 0, :], qk32[k % 2], ACT.Copy)\
                                .then_inc(m["hi_ready"], 1)
                        if n < NCH:
                            k = n
                            act.wait_ge(m["h_t_ready"], k + 1)
                            if k >= 2:
                                act.wait_ge(m["lin_qk_ready"], k - 1)
                            for b in range(2):
                                dst = ht[k % 2][0:D, :].rearrange("d (i b c) -> d i b c", b=2, c=P)[:, :, b, :]
                                mm = act.activation(dst, hT[b * D:(b + 1) * D, :]
                                                    .rearrange("d (i c) -> d i c", c=P), ACT.Copy)
                            mm.then_inc(m["h_rows_ready"], 1)

                @block.vector
                def _(dve):
                    chain = m["prologue_chain"]
                    done = [0]

                    def then(ins):
                        ins.then_inc(chain, 1)
                        done[0] += 1
                        dve.wait_ge(chain, done[0])

                    dve.wait_ge(m["exps_ready"], 1)
                    then(dve.tensor_scalar(cst[:, 0:2], ex[:, 1:3], 1.1, 1.0 / FULL, ALU.add, ALU.mult))
                    then(dve.reciprocal(cst[:, 2:4], cst[:, 0:2]))
                    then(dve.reciprocal(cst[:, 4:5], sc_in[:, ATT_SCALE:ATT_SCALE + 1]))
                    then(dve.tensor_scalar(cst[:, 5:6], cst[:, 4:5], 2.0, None, ALU.mult))
                    then(dve.tensor_tensor(cst[:, 6:7], cst[:, 5:6], sc_in[:, ATT_BIAS:ATT_BIAS + 1], ALU.add))
                    then(dve.tensor_scalar(cst[:, 5:6], cst[:, 5:6], cst[:, 0:1], cst[:, 1:2], ALU.mult, ALU.mult))
                    for c in range(2):
                        then(dve.memset(e2[:, :, c], 1.0))
                        then(dve.memset(c2[:, :, c], 1.0))
                        then(dve.tensor_scalar(c2s[:, :, c], c2[:, :, c], cst[:, 2 + c:3 + c],
                                               (-1.0, 1.0)[c], ALU.mult, ALU.mult))
                        then(dve.tensor_scalar(c2[:, :, c], c2[:, :, c], cst[:, 2 + c:3 + c], None, ALU.mult))
                        then(dve.tensor_scalar(e2[:, :, c], e2[:, :, c], ex[:, 1 + c:2 + c], None, ALU.mult))

                    for n in range(NCH + 4):
                        if n < NCH:
                            dve.wait_ge(m["sig_h_ready"], n + 1)
                            if n >= 1:
                                dve.wait_ge(m["factor_h_ready"], n)
                            dve.tensor_scalar(th[:, :], sigh[:, :], ex[:, 0:1], 1.1, ALU.mult, ALU.add)
                            then(dve.tensor_reduce(uh[:, :], sqh[:, :, 1:D], AX.X, ALU.add))
                            then(dve.tensor_scalar(uh[:, :], uh[:, :], 1e-8, None, ALU.max))
                            dve.reciprocal(uh[:, :], uh[:, :])
                            then(dve.tensor_tensor(vh[:, :], th[:, :], th[:, :], ALU.mult))
                            dve.scalar_tensor_tensor(out=vh[:, :], in0=vh[:, :], scalar=-1.0, in1=uh[:, :],
                                                     op0=ALU.add, op1=ALU.mult).then_inc(m["ratio_h_ready"], 1)
                        if 2 <= n < NCH + 2:
                            k = n - 2
                            dve.wait_ge(m["factor_qk_ready"], k + 1)
                            if k >= 2:
                                dve.wait_ge(m["hi_ready"], k - 1)
                            then(dve.tensor_tensor(gqk[:, :, :], fqk[:, :, :], c2[:, :, :], ALU.mult))
                            dve.tensor_tensor(qk32[k % 2][:, :, :, 1:D], lin_sb[k % 2][:, :, :, 1:D],
                                              gqk[:, :, :].unsqueeze(3).to_broadcast([P, CH, 2, D - 1]), ALU.mult)
                            dve.tensor_tensor(qk32[k % 2][:, :, :, 0], tqk[:, :, :], c2s[:, :, :], ALU.mult)\
                                .then_inc(m["qk_ready"], 1)
                        if n < NCH:
                            dve.wait_ge(m["factor_h_ready"], n + 1)
                            dve.tensor_tensor(h[:, n * CH:(n + 1) * CH, 1:D], lin_h[:, :, 1:D],
                                              fh[:, :].unsqueeze(2).to_broadcast([P, CH, D - 1]), ALU.mult)
                            dve.tensor_copy(h[:, n * CH:(n + 1) * CH, 0], th[:, :]).then_inc(m["h_ready"], 1)
                        if 1 <= n <= NCH:
                            k = n - 1
                            dve.wait_ge(m["sig_qk_ready"], k + 1)
                            if k >= 1:
                                dve.wait_ge(m["factor_qk_ready"], k)
                                dve.wait_ge(m["qk_ready"], k)
                            then(dve.tensor_tensor(tqk[:, :, :], sigqk[:, :, :], e2[:, :, :], ALU.mult))
                            then(dve.tensor_scalar(tqk[:, :, :], tqk[:, :, :], 1.1, None, ALU.add))
                            then(dve.tensor_reduce(uqk[:, :, :].rearrange("p t c -> p (t c)"),
                                                   sqqk[:, :, 1:D], AX.X, ALU.add))
                            then(dve.tensor_scalar(uqk[:, :, :], uqk[:, :, :], 1e-8, None, ALU.max))
                            dve.reciprocal(uqk[:, :, :], uqk[:, :, :])
                            then(dve.tensor_tensor(vqk[:, :, :], tqk[:, :, :], tqk[:, :, :], ALU.mult))
                            dve.scalar_tensor_tensor(out=vqk[:, :, :], in0=vqk[:, :, :], scalar=-1.0,
                                                     in1=uqk[:, :, :], op0=ALU.add, op1=ALU.mult)\
                                .then_inc(m["ratio_qk_ready"], 1)
                        if n >= 4:
                            k = n - 4
                            dve.wait_ge(m["stacks_a"], k + 1)
                            o = slice(k * CH * P, (k + 1) * CH * P)
                            dve.tensor_copy(q2[0:D, o], q1[D:P, o])
                            dve.tensor_copy(q2[D:P, o], q1[0:D, o])
                        if 2 <= n < NCH + 2:
                            k = n - 2
                            dve.wait_ge(m["hi_ready"], k + 1)
                            dve.tensor_tensor(parts16[k % 2][:, :, :, 1, :], qk32[k % 2],
                                              parts16[k % 2][:, :, :, 0, :], ALU.subtract).then_inc(m["lo_ready"], 1)

        prod = [sb(f"product{u}", [P, 2, S]) for u in range(2)]
        hs = sb("h_of_step", [P, T, D])
        xs = sb("x1_of_step", [P, T, D])
        sup_t = sb("support_t", [P, S])
        nb_t = sb("neighbour_t", [P, S])
        deg_p = sb("degree_parts", [P, DSLOTS, S])
        deg_s = sb("degree_sum", [P, S])
        sup_n = sb("support_nat", [P, T, D])
        wa = sb("work_a", [P, T, D])
        wb = sb("work_b", [P, T, D])
        wc = sb("work_c", [P, T, D])
        rc = sb("row_scalars", [P, 8, T])
        nat = sb("sums_nat", [P, 2, T * D + T])
        cat = sb("cat", [P, T, 2 * D])
        cat_t = sb("cat_t", [P, T, P])
        relu = sb("relu", [P, 2, T, D])
        relu_sq = sb("relu_squares", [P, T, D])
        relu_sum = sb("relu_sums", [P, 2, 2, T])
        x1_sum = sb("x1_sums", [P, NT])
        y_out = sb("y_out", [P, T, D])
        cat_psum, z_psum = sc[0], sc[1]
        x1_set = [xs, hs]

        block = ctx.enter_context(nc.Block())

        def square(idx):
            return adj_sq[bass.ds(idx, 1), :, :].rearrange("s p f -> (s p) f")

        def slot(r):
            return ring[:, r, :, :].rearrange("p t i -> p (t i)")

        def at_reg(i, n):
            return slice(i, i + n) if isinstance(i, int) else bass.ds(i, n)

        def tile_of(sl, t):
            return ring[:, bass.ds(sl, 1), t, :].rearrange("p a i -> p (a i)")

        def value(eng):
            return lambda v: v if isinstance(v, int) else eng.snap(v)

        def upper_count(eng, I):
            return eng.snap(I * (NB - 1) & (NB - 1))

        def squares_before(I):
            return I * (I - 1) >> 1

        def row_of(eng, c, second):
            snap = value(eng)
            if not second:
                return snap(c), snap(c * (NB + 1)), snap(c * (2 * NB - 1) + NB & (2 * NB - 1))
            return snap(c * (NB - 1) + (NB - 1) & (NB - 1)), snap(c * NB + NB), snap(c + 1)

        def pairs_of(eng, count):
            return value(eng)(count + 1 >> 1)

        def last_scalar(i):
            return deg_p[:, DSLOTS - 1, i * T:(i + 1) * T]


        @block.sync
        def _(sp):
            def relay(k_slot, landed):
                sp.wait_ge(slot_landed[k_slot], landed)
                sp.sem_inc(m["adj_landed"], 1)

            for r in range(HEAD, RING):
                sp.dma_start(slot(r), adj_sq[r]).then_inc(slot_landed[r], 16)
            for r in range(AHEAD):
                relay(r, 16)
            with sp.Fori(1, STEPS_A // RING) as g:
                for r in range(RING):
                    s = sp.snap(g * RING + r)
                    I = sp.snap((s >> 4) & (NB - 1))
                    at = sp.snap(I * NB + ((s + I) & (NB - 1)), min_val=0, max_val=NB * NB - 1)
                    landed = sp.snap((g + (r + AHEAD) // RING) * 16)
                    used = sp.snap((g - 1) * RING + (r + 3))
                    relay((r + AHEAD) % RING, landed)
                    sp.wait_ge(chunk_used[1], used)
                    sp.dma_start(slot(r), square(at)).then_inc(slot_landed[r], 16)
            sq = sp.alloc_register("square")
            wrap = sp.alloc_register("wrap")
            nxt = sp.alloc_register("next_row")
            late = sp.alloc_register("late")
            sp.reg_mov(sq, 0)

            def issue_b(r, at):
                sp.dma_start(slot(r), square(at)).then_inc(slot_landed[r], 16)
                sp.reg_alu(sq, sq, 1, ALU.add)
                sp.reg_alu(wrap, sq, NB - 1, ALU.bitwise_and)
                sp.reg_alu(wrap, wrap, NB - 1, ALU.add)
                sp.reg_alu(wrap, wrap, 4, ALU.logical_shift_right)
                sp.reg_alu(wrap, wrap, 1, ALU.bitwise_xor)
                sp.reg_alu(nxt, sq, 4, ALU.logical_shift_right)
                sp.reg_alu(late, nxt, NB // 2 - 1, ALU.add)
                sp.reg_alu(late, late, 4, ALU.logical_shift_right)
                sp.reg_alu(late, late, NB, ALU.add)
                sp.reg_alu(nxt, late, nxt, ALU.subtract)
                sp.reg_alu(nxt, nxt, NB + 1, ALU.mult)
                sp.reg_alu(nxt, nxt, sq, ALU.subtract)
                sp.reg_alu(nxt, nxt, wrap, ALU.mult)
                sp.reg_alu(sq, sq, nxt, ALU.add)

            ga = STEPS_A // RING
            for r in range(RING):
                relay((r + AHEAD) % RING, 16 * (ga + (r + AHEAD) // RING))
                sp.wait_ge(chunk_used[1], min((ga - 1) * RING + r + 3, STEPS_A + 1))
                if r == RING - 1:
                    sp.wait_ge(m["deg_reduced"], LOWER)
                issue_b(r, sp.snap(sq, min_val=0, max_val=NB * NB - 1))
            with sp.Fori(0, STEPS_B // RING - 1) as g:
                for r in range(RING):
                    at = sp.snap(sq, min_val=0, max_val=NB * NB - 1)
                    landed = sp.snap((g + (ga + 1) + (r + AHEAD) // RING) * 16)
                    used = sp.snap(g * RING + (r + 3))
                    relay((r + AHEAD) % RING, landed)
                    sp.wait_ge(b_used[1], used)
                    sp.wait_ge(m["deg_added_b"], used)
                    issue_b(r, at)
            for r in range(AHEAD, RING):
                relay(r, 16 * (STEPS_A + STEPS_B) // RING)
            sp.wait_ge(m["last_ready"], 1)
            sp.dma_start(out[NB // 2], deg_p[:, 2, 0:T * D]).then_inc(m["last_stored"], 16)
            sp.wait_ge(m["last_stored"], 16)

        @block.tensor
        def _(pe):
            def scores(s1, kcol, qcol, u):
                for t in (2 * u, 2 * u + 1):
                    pe.wait_ge(prod_ready[t], s1)
                    w = kst[:, bass.ds(kcol + t * P, P)]
                    pe.matmul(sc[t][:, :], w, q1[:, bass.ds(qcol, S)], start=True, stop=False)
                    pe.matmul(sc[t][:, :], w, q2[:, bass.ds(qcol, S)], start=False, stop=True)\
                        .then_inc(scores_ready[t], 1)

            def columns(s1):
                I1 = pe.snap((s1 >> 4) & (NB - 1))
                return pe.snap(((s1 + I1) & (NB - 1)) * S), pe.snap(I1 * S)

            def add_to(acc, lhs, rhs):
                return pe.matmul(acc, lhs, rhs, start=False, stop=False, skip_group_check=True)

            def support(u, t, half_):
                return add_to(acc_sup[D * half_:D * half_ + D, :], hs[:, t, :], prod[u][:, t % 2, :])

            def zero(acc):
                pe.matmul(acc[:, :], zero16[:, 0:P], zero16[:, :], start=True, stop=False, skip_group_check=True)

            def upper(s1, ends=None):
                kcol, qcol = columns(s1)
                for u in range(2):
                    scores(s1, kcol, qcol, u)
                    if u == 0 and ends:
                        take(*ends)
                    pe.wait_ge(values_ready[u], s1)
                    support(u, 2 * u, 0)
                    support(u, 2 * u + 1, 1).then_inc(chunk_used[u], 1)

            def lower(s1):
                kcol, qcol = columns(s1)
                sl = pe.snap((s1 - 1) & (RING - 1))
                for u in range(2):
                    scores(s1, kcol, qcol, u)
                    pe.wait_ge(values_ready[u], s1)
                    for t in (2 * u, 2 * u + 1):
                        add_to(acc_nb[0:D, :], xs[:, t, :], tile_of(sl, t))
                        mm = support(u, t, 1)
                    mm.then_inc(chunk_used[u], 1)

            def take(I, has_lower):
                pe.wait_ge(m["sup_t_ready"], I + 1)
                zero(acc_sup)
                if has_lower:
                    pe.wait_ge(m["nb_t_ready"], I)
                    zero(acc_nb)

            def turn(I, has_lower):
                pe.wait_ge(m["sup_saved"], I + 1)
                for c in range(T):
                    mm = pe.matmul(misc[:, c * D:(c + 1) * D], sup_t[:, c * P:(c + 1) * P], fold[:, :],
                                   start=True, stop=True)
                mm.then_inc(m["sup_nat_ready"], 1)
                if has_lower:
                    pe.wait_ge(m["nb_saved"], I)
                    pe.wait_ge(m["deg_s_ready"], I)
                    for c in range(T):
                        o = slice(c * P, (c + 1) * P)
                        pe.matmul(acc_deg[:, c * D:(c + 1) * D], nb_t[0:D, o], fold[0:D, :], start=True, stop=True)
                        mm = pe.matmul(acc_deg[:, T * D + c:T * D + c + 1], deg_s[:, o], ones[:, 0:1],
                                       start=True, stop=True)
                    mm.then_inc(m["nb_nat_ready"], 1)

            for u in range(2):
                pe.sem_inc(chunk_used[u], 1)
                pe.sem_inc(b_used[u], 2)
            pe.sem_inc(m["cat_t_psum"], 1)
            zero(acc_sup)
            zero(acc_nb)
            for t in range(T):
                w = kst[:, t * P:(t + 1) * P]
                pe.matmul(sc[t][:, :], w, q1[:, 0:S], start=True, stop=False)
                pe.matmul(sc[t][:, :], w, q2[:, 0:S], start=False, stop=True).then_inc(scores_ready[t], 1)
            with pe.Fori(0, NB) as d:
                upper(pe.snap(d + 1))

            def row_block(I, is_first, is_last):
                uppers = upper_count(pe, I)
                before = 0 if is_first else pe.snap(I + (NB - 1) & (NB - 1))
                upper(pe.snap(I * NB + 1), (before, not is_first))
                turn(before, not is_first)
                if not is_last:
                    with pe.Fori(1, uppers) as d:
                        upper(pe.snap(I * NB + d + 1))
                with pe.Fori(0, I) as J:
                    lower(pe.snap(I * NB + uppers + J + 1))

            with pe.Fori(1, 2) as I:
                row_block(I, True, False)
            with pe.Fori(2, NB - 1) as I:
                row_block(I, False, False)
            with pe.Fori(NB - 1, NB) as I:
                row_block(I, False, True)
            take(NB - 1, True)
            turn(NB - 1, True)
            pe.sem_inc(m["b_nat_ready"], 1)

            def add_square(n, h_):
                sl = pe.snap(n & (RING - 1))
                for u in range(2):
                    pe.wait_ge(b_static[u], n + 1)
                    add_to(acc_nb[0:D, :], x1_set[h_][:, 2 * u, :], tile_of(sl, 2 * u))
                    add_to(acc_nb[D:P, :], x1_set[h_][:, 2 * u + 1, :], prod[u][:, h_, :])\
                        .then_inc(b_used[u], 1)

            def squares(n0, count, first, end):
                with pe.Fori(first, end) as g:
                    n = pe.snap(n0 + g * 2)
                    add_square(n, 0)
                    with pe.If(pe.snap(g * 2 + 1) < count):
                        add_square(pe.snap(n + 1), 1)

            def turn_sums(K):
                pe.wait_ge(m["b_nb_t_ready"], K + 1)
                pe.wait_ge(m["b_nat_saved"], K + 1)
                for t in range(T):
                    pe.matmul(misc[:, t * D:(t + 1) * D], nb_t[:, t * P:(t + 1) * P], fold[:, :],
                              start=True, stop=True)
                zero(acc_nb)

            def turn_degrees(K):
                pe.wait_ge(m["b_deg_s_ready"], K + 1)
                for t in range(T):
                    mm = pe.matmul(misc[:, T * D + t:T * D + t + 1], deg_s[:, t * P:(t + 1) * P], ones[:, 0:1],
                                   start=True, stop=True)
                mm.then_inc(m["b_nat_ready"], 1)

            def turn_cat(done):
                pe.wait_ge(m["cat_ready"], done)
                for t in range(T):
                    mm = pe.transpose(cat_psum[:, t * P:(t + 1) * P], cat[:, t, :], ident[:, :])
                mm.then_inc(m["cat_t_psum"], 1)

            def linear(done):
                pe.wait_ge(m["cat_t_ready"], done)
                pe.matmul(z_psum[:, 0:T * D], ones[0:1, :], b1_sb[:, :], start=True, stop=False,
                          skip_group_check=True)
                for t in range(T):
                    mm = pe.matmul(z_psum[:, t * D:(t + 1) * D], cat_t[:, t, :], w1_sb[:, :], start=False,
                                   stop=t == T - 1, skip_group_check=True)
                mm.then_inc(m["z_ready"], 1)

            def sum_row(c, second, is_first=False):
                K = value(pe)(c * 2 + second)
                _, n0, count = row_of(pe, c, second)
                squares(n0, count, 0, pairs_of(pe, count))
                turn_sums(K)
                if not is_first:
                    turn_cat(K)
                    linear(K)
                turn_degrees(K)

            def sum_last_row():
                c = NB // 2 - 1
                _, n0, count = row_of(pe, c, 1)
                pairs = pairs_of(pe, count)
                squares(n0, count, 0, pairs // 2)
                turn_cat(NB - 1)
                squares(n0, count, pairs // 2, pairs - 1)
                linear(NB - 1)
                squares(n0, count, pairs - 1, pairs)
                turn_sums(NB - 1)
                turn_degrees(NB - 1)
                turn_cat(NB)
                linear(NB)

            sum_row(0, 0, is_first=True)
            sum_row(0, 1)
            with pe.Fori(1, NB // 2 - 1) as c:
                sum_row(c, 0)
                sum_row(c, 1)
            sum_row(NB // 2 - 1, 0)
            sum_last_row()

        @block.scalar
        def _(act):
            def sigmoids(s1, u):
                for t in (2 * u, 2 * u + 1):
                    act.wait_ge(scores_ready[t], s1 + 1)
                    act.activation(sc[t][:, :], sc[t][:, :], ACT.Sigmoid, bias=cst[:, 6:7],
                                   scale=cst[:, 5:6]).then_inc(att_ready[t], 1)

            def step(s, J, with_x1):
                j = value(act)(J * T)
                for u in range(2):
                    half_of = slice(2 * u, 2 * u + 2)
                    act.wait_ge(chunk_used[u], s + 1)
                    if with_x1:
                        if u == 0:
                            act.wait_ge(m["x1_ready"], J + 2)
                        act.activation(xs[:, half_of, :], xn[:, bass.ds(j + 2 * u, 2), :], ACT.Copy)
                    act.activation(hs[:, half_of, :], h[:, bass.ds(j + 2 * u, 2), :], ACT.Copy)\
                        .then_inc(values_ready[u], 1)
                    sigmoids(s + 1, u)

            def take(I, has_lower):
                act.wait_ge(chunk_used[1], I * NB + (NB + 1))
                act.activation(sup_t[:, :], acc_sup[:, :], ACT.Copy).then_inc(m["sup_t_ready"], 1)
                if has_lower:
                    act.activation(nb_t[0:D, :], acc_nb[0:D, :], ACT.Copy).then_inc(m["nb_t_ready"], 1)

            def save(I, has_lower):
                act.wait_ge(m["sup_nat_ready"], I + 1)
                act.wait_ge(m["x1_ready"], I + 1)
                act.activation(sup_n[:, :, :], misc[:, 0:T * D].rearrange("p (t d) -> p t d", d=D), ACT.Copy)\
                    .then_inc(m["sup_saved"], 1)
                if has_lower:
                    act.wait_ge(m["nb_nat_ready"], I)
                    act.activation(nb_a[:, bass.ds(I * T, T), :],
                                   acc_deg[:, 0:T * D].rearrange("p (t d) -> p t d", d=D), ACT.Copy)
                    act.activation(deg_a[:, bass.ds(I * T, T)], acc_deg[:, T * D:T * D + T], ACT.Copy)\
                        .then_inc(m["nb_saved"], 1)

            act.sem_inc(m["sup_saved"], 1)
            act.sem_inc(m["b_nat_saved"], 1)
            act.sem_inc(m["nb_saved"], 1)
            act.sem_inc(m["relu_part"], T)
            sigmoids(0, 0)
            sigmoids(0, 1)
            with act.Fori(0, NB) as J:
                step(J, J, False)
            take(0, False)

            def row_block(I, is_first, is_last):
                uppers = upper_count(act, I)
                step(act.snap(I * NB), I, False)
                save(0 if is_first else act.snap(I + (NB - 1) & (NB - 1)), not is_first)
                if not is_last:
                    with act.Fori(1, uppers) as d:
                        step(act.snap(I * NB + d), act.snap((I + d) & (NB - 1)), False)
                with act.Fori(0, I) as J:
                    step(act.snap(I * NB + uppers + J), J, True)
                take(I, True)

            with act.Fori(1, 2) as I:
                row_block(I, True, False)
            with act.Fori(2, NB - 1) as I:
                row_block(I, False, False)
            with act.Fori(NB - 1, NB) as I:
                row_block(I, False, True)
            save(NB - 1, True)

            def copy_square(n, J, h_):
                sl = act.snap(n & (RING - 1))
                jt = act.snap(J * T)
                act.wait_ge(m["adj_landed"], n + (STEPS_A + 1))
                act.wait_ge(m["x1_ready"], J + 2)
                for u in range(2):
                    act.wait_ge(b_used[u], n + 1)
                    act.activation(x1_set[h_][:, 2 * u:2 * u + 2, :], xn[:, bass.ds(jt + 2 * u, 2), :], ACT.Copy)
                    act.activation(prod[u][:, h_, :], tile_of(sl, 2 * u + 1), ACT.Copy)\
                        .then_inc(b_static[u], 1)

            def squares(I, n0, count, first, end):
                with act.Fori(first, end) as g:
                    n = act.snap(n0 + g * 2)
                    d = act.snap(g * 2)
                    copy_square(n, act.snap((I + d) & (NB - 1)), 0)
                    with act.If(d + 1 < count):
                        copy_square(act.snap(n + 1), act.snap((I + d + 1) & (NB - 1)), 1)

            def take_sums(n0, count):
                act.wait_ge(b_used[1], n0 + count + 2)
                act.activation(nb_t[:, :], acc_nb[:, :], ACT.Copy).then_inc(m["b_nb_t_ready"], 1)

            def save_sums(K, second):
                act.wait_ge(m["b_nat_ready"], K + 2)
                act.wait_ge(m["nat_read"], K + 1)
                act.activation(nat[:, second, :], misc[:, 0:T * D + T], ACT.Copy).then_inc(m["b_nat_saved"], 1)

            def save_cat(done):
                act.wait_ge(m["cat_t_psum"], done + 1)
                act.activation(cat_t[:, :, :], cat_psum[:, :].rearrange("p (t i) -> p t i", t=T), ACT.Copy)\
                    .then_inc(m["cat_t_ready"], 1)

            def relu_row(done, second):
                act.wait_ge(m["z_ready"], done)
                act.wait_ge(m["out_ready"], done)
                for t in range(T):
                    act.activation(relu[:, second, t, :], z_psum[:, t * D:(t + 1) * D], ACT.Relu,
                                   accum_out=relu_sum[:, second, 0, t:t + 1]).then_inc(m["relu_part"], 1)
                for t in range(T):
                    act.wait_ge(m["relu_part"], done * T + (t + 1))
                    mm = act.activation(relu_sq[:, t, :], relu[:, second, t, :], ACT.Square,
                                        accum_out=relu_sum[:, second, 1, t:t + 1])
                mm.then_inc(m["relu_ready"], 1)

            def sum_row(c, second, before=2):
                K = value(act)(c * 2 + second)
                I, n0, count = row_of(act, c, second)
                pairs = pairs_of(act, count)
                squares(I, n0, count, 0, 1)
                if before >= 1:
                    save_sums(K + (2 * NB - 1) & (2 * NB - 1), 1 - second)
                if before >= 2:
                    relu_row(K + (2 * NB - 1) & (2 * NB - 1), second)
                if not isinstance(pairs, int):
                    with act.If(pairs > 1):
                        squares(I, n0, count, 1, pairs)
                elif pairs > 1:
                    squares(I, n0, count, 1, pairs)
                take_sums(n0, count)
                if before >= 1:
                    save_cat(K)

            def sum_last_row():
                c, K = NB // 2 - 1, NB - 1
                I, n0, count = row_of(act, c, 1)
                pairs = pairs_of(act, count)
                squares(I, n0, count, 0, 1)
                save_sums(K - 1, 0)
                relu_row(K - 1, 1)
                squares(I, n0, count, 1, pairs // 2)
                squares(I, n0, count, pairs // 2, pairs - 1)
                save_cat(NB - 1)
                squares(I, n0, count, pairs - 1, pairs)
                relu_row(NB - 1, 0)
                take_sums(n0, count)
                save_sums(K, 1)
                save_cat(NB)
                relu_row(NB, 1)

            sum_row(0, 0, before=0)
            sum_row(0, 1, before=1)
            with act.Fori(1, NB // 2 - 1) as c:
                sum_row(c, 0)
                sum_row(c, 1)
            sum_row(NB // 2 - 1, 0)
            sum_last_row()

        @block.vector
        def _(dve):
            def product(s, sl, u):
                dve.wait_ge(chunk_used[u], s + 1)
                for t in (2 * u, 2 * u + 1):
                    dve.wait_ge(att_ready[t], s + 1)
                    dve.tensor_tensor(prod[u][:, t % 2, :], sc[t][:, :], tile_of(sl, t), ALU.mult)\
                        .then_inc(prod_ready[t], 1)

            def degrees(sl, part, lo=0, hi=S):
                return dve.tensor_reduce(deg_p[:, bass.ds(part, 1), lo:hi].rearrange("p a i -> p (a i)"),
                                         ring[:, bass.ds(sl, 1), :, lo:hi].rearrange("p a t i -> p i (a t)"),
                                         AX.X, ALU.add)

            def upper(s):
                sl = dve.snap(s & (RING - 1))
                dve.wait_ge(m["adj_landed"], s + 1)
                for u in range(2):
                    product(s, sl, u)

            with dve.Fori(0, NB) as J:
                upper(J)
            with dve.Fori(1, NB) as I:
                uppers = upper_count(dve, I)
                with dve.Fori(0, uppers) as d:
                    upper(dve.snap(I * NB + d))
                with dve.Fori(0, I) as J:
                    s = dve.snap(I * NB + uppers + J)
                    n = dve.snap(squares_before(I) + J)
                    sl = dve.snap(s & (RING - 1))
                    part = dve.snap(n & (DSLOTS - 1))
                    dve.wait_ge(m["adj_landed"], s + 1)
                    product(s, sl, 0)
                    dve.wait_ge(m["deg_added"], n + 1)
                    degrees(sl, part, 0, S // 2)
                    product(s, sl, 1)
                    degrees(sl, part, S // 2, S).then_inc(m["deg_reduced"], 1)

            deg_acc = deg_p

            def whole(n):
                return ring[:, bass.ds(n & (RING - 1), 1), :, :].rearrange("p a t i -> p (a t) i")

            def degree_row(c, second):
                K = value(dve)(c * 2 + second)
                _, n0, count = row_of(dve, c, second)
                dve.drain()
                dve.wait_ge(m["adj_landed"], n0 + (STEPS_A + 1))
                dve.tensor_copy(deg_acc[:, :, :], whole(n0)).then_inc(m["deg_added_b"], 1)
                with dve.Fori(1, count + 1) as d:
                    with dve.If(d < count):
                        n = dve.snap(n0 + d)
                        dve.wait_ge(m["adj_landed"], n + (STEPS_A + 1))
                        dve.wait_ge(m["deg_added_b"], n + 2)
                        dve.tensor_tensor(deg_acc[:, :, :], deg_acc[:, :, :], whole(n), ALU.add)\
                            .then_inc(m["deg_added_b"], 1)
                dve.wait_ge(m["deg_added_b"], n0 + count + 2)
                dve.wait_ge(m["b_nat_ready"], K + 1)
                dve.tensor_reduce(deg_s[:, :], deg_acc[:, :, :].rearrange("p t i -> p i t"), AX.X, ALU.add)\
                    .then_inc(m["b_deg_s_ready"], 1)

            dve.sem_inc(m["deg_added_b"], 2)
            dve.wait_ge(m["deg_added"], DSLOTS + LOWER)
            with dve.Fori(0, NB // 2) as c:
                degree_row(c, 0)
                degree_row(c, 1)

            K, I = NB - 1, NB // 2
            x_blk = xn[:, I * T:(I + 1) * T, :]

            def room(i):
                return deg_p[:, i, 0:T * D].rearrange("p (t d) -> p t d", d=D)

            def over_d(a):
                return a.unsqueeze(2).to_broadcast([P, T, D])

            done = [0]

            def then(ins):
                ins.then_inc(m["last_chain"], 1)
                done[0] += 1
                dve.wait_ge(m["last_chain"], done[0])

            dve.wait_ge(m["b_deg_s_ready"], NB)
            dve.wait_ge(m["cat_t_psum"], NB)
            dve.tensor_copy(cat[:, :, 0:D], x_blk)
            then(dve.tensor_tensor(room(0), nb_a[:, I * T:(I + 1) * T, :], x_blk, ALU.add))
            dve.wait_ge(m["b_nat_saved"], NB + 1)
            dve.tensor_tensor(room(0), room(0), nat[:, 1, 0:T * D].rearrange("p (t d) -> p t d", d=D), ALU.add)
            then(dve.scalar_tensor_tensor(out=last_scalar(0), in0=nat[:, 1, T * D:T * D + T], scalar=1.0,
                                          in1=deg_a[:, I * T:(I + 1) * T], op0=ALU.add, op1=ALU.add))
            then(dve.tensor_scalar(last_scalar(0), last_scalar(0), 1.0, None, ALU.max))
            then(dve.reciprocal(last_scalar(1), last_scalar(0)))
            dve.tensor_tensor(cat[:, :, D:2 * D], room(0), over_d(last_scalar(1)), ALU.mult).then_inc(m["cat_ready"], 1)
            dve.wait_ge(m["relu_ready"], NB)
            dve.tensor_scalar(last_scalar(2), relu_sum[:, 1, 1, :], 1e-24, None, ALU.max).then_inc(m["last_base"], 1)
            dve.wait_ge(m["last_root"], 1)
            then(dve.tensor_tensor(room(1), relu[:, 1, :, :], over_d(last_scalar(3)), ALU.mult))
            then(dve.tensor_tensor(room(1), room(1), x_blk, ALU.add))
            then(dve.tensor_reduce(last_scalar(4), room(1), AX.X, ALU.add))
            then(dve.tensor_scalar(last_scalar(4), last_scalar(4), 1.0 / D, None, ALU.mult))
            then(dve.tensor_tensor(room(1), room(1), over_d(last_scalar(4)), ALU.subtract))
            then(dve.tensor_tensor(room(0), room(1), room(1), ALU.mult))
            then(dve.tensor_reduce(last_scalar(5), room(0), AX.X, ALU.add))
            dve.tensor_scalar(last_scalar(5), last_scalar(5), 1.0 / D, EPS, ALU.mult, ALU.add).then_inc(m["last_base"], 1)
            dve.wait_ge(m["last_root"], 2)
            dve.tensor_tensor(room(2), room(1), over_d(last_scalar(6)), ALU.mult).then_inc(m["last_ready"], 1)

        @block.gpsimd
        def _(pool):
            def then(ins):
                pool.drain()

            def row(i):
                return rc[:, i, :]

            def spread(i):
                return rc[:, i, :].unsqueeze(2).to_broadcast([P, T, D])

            def row_sum(buf, out_row):
                w = D // 2
                while w >= 1:
                    dst = buf[:, :, 0:w] if w > 1 else row(out_row).unsqueeze(2)
                    then(pool.tensor_tensor(dst, buf[:, :, 0:w], buf[:, :, w:2 * w], ALU.add))
                    w //= 2

            def kept_sum(src, out_):
                w = D // 2
                then(pool.tensor_tensor(wb[:, :, 0:w], src[:, :, 0:w], src[:, :, w:D], ALU.add))
                while w > 1:
                    w //= 2
                    dst = wb[:, :, 0:w] if w > 1 else out_.unsqueeze(2)
                    then(pool.tensor_tensor(dst, wb[:, :, 0:w], wb[:, :, w:2 * w], ALU.add))

            def layernorm(src, last_out):
                then(pool.tensor_scalar(row(1), row(0), 1.0 / D, None, ALU.mult))
                then(pool.tensor_tensor(wc[:, :, :], src, spread(1), ALU.subtract))
                then(pool.tensor_tensor(wb[:, :, :], wc[:, :, :], wc[:, :, :], ALU.mult))
                row_sum(wb, 2)
                then(pool.tensor_scalar(row(3), row(2), 1.0 / D, EPS, ALU.mult, ALU.add))
                then(pool.tensor_tensor(row(4), row(3), half[:, 0:T], ALU.pow))
                return pool.tensor_tensor(last_out, wc[:, :, :], spread(4), ALU.mult)

            def finish_x1(I):
                x_blk = xn[:, at_reg(I * T, T), :]
                pool.wait_ge(m["sup_saved"], I + 2)
                then(pool.tensor_tensor(wa[:, :, :], sup_n[:, :, :], sup_n[:, :, :], ALU.mult))
                then(pool.tensor_scalar(row(5), wa[:, :, 0], -2.0, None, ALU.mult))
                row_sum(wa, 6)
                then(pool.tensor_tensor(row(5), row(5), row(6), ALU.add))
                pool.tensor_scalar(row(6), row(5), 0.0, None, ALU.max)
                then(pool.tensor_scalar(row(7), row(5), 0.0, None, ALU.min))
                then(pool.tensor_tensor(row(6), row(6), row(7), ALU.subtract))
                then(pool.tensor_scalar(row(6), row(6), 1e-8, None, ALU.max))
                then(pool.tensor_tensor(row(5), row(6), half[:, 0:T], ALU.pow))
                then(pool.tensor_tensor(wa[:, :, :], sup_n[:, :, :], spread(5), ALU.mult))
                then(pool.tensor_tensor(wa[:, :, :], wa[:, :, :], x_blk, ALU.add))
                kept_sum(wa[:, :, :], row(0))
                layernorm(wa[:, :, :], x_blk).then_inc(m["x1_ready"], 1)
                pool.drain()
                kept_sum(x_blk, x1_sum[:, at_reg(I * T, T)])

            pool.sem_inc(m["x1_ready"], 1)
            pool.sem_inc(m["nat_read"], 2)
            pool.sem_inc(m["out_ready"], 2)
            pool.sem_inc(m["deg_added"], DSLOTS)
            finish_x1(0)
            with pool.Fori(1, NB) as I:
                pool.wait_ge(m["nb_saved"], I)
                pool.sem_inc(m["deg_seen"], 1)
                pool.memset(deg_s[:, :], 0.0)
                pool.drain()
                with pool.Fori(0, I) as J:
                    n = pool.snap(squares_before(I) + J)
                    pool.wait_ge(m["deg_reduced"], n + 1)
                    pool.sem_inc(m["deg_seen"], 1)
                    pool.tensor_tensor(deg_s[:, :], deg_s[:, :],
                                       deg_p[:, bass.ds(n & (DSLOTS - 1), 1), :].rearrange("p a i -> p (a i)"),
                                       ALU.add).then_inc(m["deg_added"], 1)
                    pool.drain()
                pool.sem_inc(m["deg_s_ready"], 1)
                finish_x1(I)

            def neighbours(done, I, second):
                x_blk = xn[:, at_reg(I * T, T), :]
                pool.wait_ge(m["cat_t_psum"], done)
                pool.wait_ge(m["b_nat_saved"], done + 1)
                pool.tensor_tensor(row(0), nat[:, second, T * D:T * D + T], one4[:, :], ALU.add)
                pool.tensor_tensor(cat[:, :, 0:D], x_blk, zero4[:, :].unsqueeze(2).to_broadcast([P, T, D]), ALU.add)
                then(pool.tensor_tensor(wa[:, :, :], nat[:, second, 0:T * D].rearrange("p (t d) -> p t d", d=D),
                                        nb_a[:, at_reg(I * T, T), :], ALU.add))
                pool.sem_inc(m["nat_read"], 1)
                then(pool.tensor_tensor(row(0), row(0), deg_a[:, at_reg(I * T, T)], ALU.add))
                pool.tensor_tensor(wa[:, :, :], wa[:, :, :], x_blk, ALU.add)
                then(pool.tensor_scalar(row(0), row(0), 1.0, None, ALU.max))
                then(pool.tensor_tensor(row(1), row(0), minus_one[:, :], ALU.pow))
                pool.tensor_tensor(cat[:, :, D:2 * D], wa[:, :, :], spread(1), ALU.mult)\
                    .then_inc(m["cat_ready"], 1)
                pool.drain()

            def finish_x2(done, I, stored, second):
                pool.wait_ge(m["relu_ready"], done)
                pool.sem_inc(m["relu_seen"], 1)
                then(pool.tensor_scalar(row(6), relu_sum[:, second, 1, :], 1e-24, None, ALU.max))
                then(pool.tensor_tensor(row(7), row(6), half[:, 0:T], ALU.pow))
                pool.tensor_tensor(row(0), relu_sum[:, second, 0, :], row(7), ALU.mult)
                then(pool.tensor_tensor(wa[:, :, :], relu[:, second, :, :], spread(7), ALU.mult))
                pool.tensor_tensor(row(0), row(0), x1_sum[:, at_reg(I * T, T)], ALU.add)
                then(pool.tensor_tensor(wa[:, :, :], wa[:, :, :], xn[:, at_reg(I * T, T), :], ALU.add))
                if stored is not None:
                    pool.wait_ge(m["out_stored"], stored * 16)
                    pool.sem_inc(m["stored_seen"], 1)
                layernorm(wa[:, :, :], y_out[:, :, :]).then_inc(m["out_ready"], 1)
                pool.drain()
                pool.dma_start(out[at_reg(I, 1), :, :].rearrange("s p f -> (s p) f"),
                               y_out[:, :, :].rearrange("p t d -> p (t d)")).then_inc(m["out_stored"], 16)

            neighbours(1, 0, 0)
            neighbours(2, NB - 1, 1)
            finish_x2(1, 0, None, 0)
            with pool.Fori(0, NB // 2 - 2) as b:
                c = pool.snap(b + 1)
                before = pool.snap(b * (NB - 1) + (NB - 1) & (NB - 1))
                small = pool.snap(b * (NB - 1) + (NB - 2) & (NB - 1))
                neighbours(pool.snap(b * 2 + 3), c, 0)
                finish_x2(pool.snap(b * 2 + 2), before, pool.snap(b * 2 + 1), 1)
                neighbours(pool.snap(b * 2 + 4), small, 1)
                finish_x2(pool.snap(b * 2 + 3), c, pool.snap(b * 2 + 2), 0)
            neighbours(NB - 1, NB // 2 - 1, 0)
            finish_x2(NB - 2, NB // 2 + 1, NB - 3, 1)
            finish_x2(NB - 1, NB // 2 - 1, NB - 2, 0)
            for k, (dst, base) in enumerate(((3, 2), (6, 5))):
                pool.wait_ge(m["last_base"], k + 1)
                pool.tensor_tensor(last_scalar(dst), last_scalar(base), half[:, 0:T], ALU.pow).then_inc(m["last_root"], 1)
            pool.wait_ge(m["out_stored"], (NB - 1) * 16)
            pool.sem_inc(m["stored_seen"], 1)


def kernel(x, adj, L0_gnn_W, L0_gnn_b, L0_gnn_scale, L0_gnn_Wq, L0_gnn_bq, L0_gnn_scale_q, L0_gnn_Wk, L0_gnn_bk,
           L0_gnn_scale_k, L0_gnn_att_bias, L0_gnn_att_scale, L1_gnn_W, L1_gnn_b):
    import numpy as np
    import concourse.bacc as bacc
    from concourse.bass_utils import run_bass_kernel_spmd

    nc = bacc.Bacc("TRN2", target_bir_lowering=False, num_devices=1)
    x = np.asarray(x)
    scalars = np.stack([np.asarray(v).reshape(()) for v in
                        (L0_gnn_scale, L0_gnn_scale_q, L0_gnn_scale_k, L0_gnn_att_bias, L0_gnn_att_scale)])
    arrays = {
        "adj_sq": np.ascontiguousarray(np.asarray(adj).reshape(NB, S, NB, T, P).transpose(0, 2, 4, 3, 1))
        .reshape(NB * NB, P, T * S),
        "x_nat": np.ascontiguousarray(x.reshape(NT, P, D).transpose(1, 0, 2)),
        "x_t": np.concatenate([x.T, np.ones((1, N), x.dtype)]),
        "w_t": np.concatenate([np.asarray(L0_gnn_W).T, np.asarray(L0_gnn_b)[None]]),
        "wqk_t": np.concatenate([np.concatenate([np.asarray(L0_gnn_Wq).T, np.asarray(L0_gnn_Wk).T], 1),
                                 np.concatenate([np.asarray(L0_gnn_bq), np.asarray(L0_gnn_bk)])[None]]),
        "w1": np.ascontiguousarray(np.asarray(L1_gnn_W)),
        "b1": np.ascontiguousarray(np.tile(np.asarray(L1_gnn_b).reshape(1, D), (1, T))),
        "scalars": np.ascontiguousarray(np.broadcast_to(scalars[None], (P, 5))),
    }
    args = [nc.dram_tensor(n, a.shape, F32, kind="ExternalInput").ap() for n, a in arrays.items()]
    out = nc.dram_tensor("x2", (NB, P, T * D), F32, kind="ExternalOutput").ap()
    two_layers(nc, *args, out)
    got = run_bass_kernel_spmd(nc, [arrays], core_ids=[0]).results[0]["x2"]
    return np.ascontiguousarray(np.asarray(got).reshape(NB, P, T, D).transpose(0, 2, 1, 3)).reshape(N, D)
```
